# Optimizing a Trainium2 kernel written in Bass

```python
import numpy as np
import jax
import jax.numpy as jnp

def _softmax(x, axis=-1):
    return jax.nn.softmax(x, axis=axis)

def _gelu(x):
    return jax.nn.gelu(x, approximate=True)

def _silu(x):
    return jax.nn.silu(x)

def _sigmoid(x):
    return jax.nn.sigmoid(x)

def _layernorm(x, axis=-1, eps=1e-05):
    m = jnp.mean(x, axis=axis, keepdims=True)
    v = jnp.var(x, axis=axis, keepdims=True)
    return (x - m) / jnp.sqrt(v + eps)

def _scatter_add(tgt, idx, src, axis=0):
    return tgt.at[idx].add(src)

def _segment_sum(src, seg, n):
    return jax.ops.segment_sum(src, seg, n)
kernel_name = 'mk_audio_tower_d1_tok_audfeat2048_r4_64c16b'

def setup_inputs(seed: int=0):
    np.random.seed(seed)
    _w = jnp.asarray

    def _rec_inputs():
        import jax
        import jax.numpy as jnp
        _rk = jax.random.key(seed)
        x = 0.000106427 + 1.00001 * jax.random.normal(jax.random.fold_in(_rk, 1), (64, 96, 512), jnp.float32)
        return x
    x = _rec_inputs()

    def _L0_tok_setup():
        import jax, jax.numpy as jnp
        import numpy as np
        key = jax.random.key(seed)
        N, C, T = (64, 128, 512)
        qkv = jax.random.normal(key, (N, 3 * C, T), dtype=jnp.float32)
        return {'qkv': qkv}
    _L0_tok_all = _L0_tok_setup()
    _L0_tok_in = {k: v for k, v in _L0_tok_all.items() if k in ()}
    del _L0_tok_all

    def _L0_attn_setup():
        import jax, jax.numpy as jnp
        import numpy as np
        HEADS, KV_HEADS, HEAD_DIM = (16, 4, 128)
        WINDOW, ROPE_THETA, EPS = (128, 10000.0, 1e-06)

        def _rms_norm(x, w):
            xf = x.astype(jnp.float32)
            y = xf * jax.lax.rsqrt(jnp.mean(xf * xf, axis=-1, keepdims=True) + EPS)
            return (y * (1.0 + w.astype(jnp.float32))).astype(x.dtype)

        def _rope_cos_sin(T, dtype):
            inv_freq = 1.0 / ROPE_THETA ** (jnp.arange(0, HEAD_DIM, 2, dtype=jnp.float32) / HEAD_DIM)
            pos = jnp.arange(T, dtype=jnp.float32)
            freqs = pos[:, None] * inv_freq[None, :]
            emb = jnp.concatenate([freqs, freqs], axis=-1)
            return (emb.astype(dtype), emb)

        def _rotate_half(x):
            x1, x2 = jnp.split(x, 2, axis=-1)
            return jnp.concatenate([-x2, x1], axis=-1)
        key = jax.random.key(seed)
        ks = jax.random.split(key, 7)
        B, T, D = (2, 512, 512)
        s = lambda k, shape, fan: jax.random.normal(k, shape, jnp.float32) * fan ** (-0.5)
        return {'x': jax.random.normal(ks[0], (B, T, D), jnp.float32), 'Wq': s(ks[1], (HEADS * HEAD_DIM, D), D), 'Wk': s(ks[2], (KV_HEADS * HEAD_DIM, D), D), 'Wv': s(ks[3], (KV_HEADS * HEAD_DIM, D), D), 'Wo': s(ks[4], (D, HEADS * HEAD_DIM), HEADS * HEAD_DIM), 'qn_w': jax.random.normal(ks[5], (HEAD_DIM,), jnp.float32) * 0.02, 'kn_w': jax.random.normal(ks[6], (HEAD_DIM,), jnp.float32) * 0.02}
    _L0_attn_all = _L0_attn_setup()
    _L0_attn_in = {k: v for k, v in _L0_attn_all.items() if k in ('Wq', 'Wk', 'Wv', 'Wo', 'qn_w', 'kn_w')}
    del _L0_attn_all

    def _L0_ffn_setup():
        import jax, jax.numpy as jnp
        import numpy as np
        EPS = 1e-08

        def _quantize(w):
            gamma = jnp.mean(jnp.abs(w))
            return jnp.clip(jnp.round(w / (gamma + EPS)), -1.0, 1.0)

        def _bitlinear(x, w):
            return jnp.matmul(x, _quantize(w).T)
        key = jax.random.key(seed)
        k1, k2, k3, k4 = jax.random.split(key, 4)
        d, h = (512, 1408)
        x = jax.random.normal(k1, (4, 512, d), dtype=jnp.float32)
        w1 = jax.random.normal(k2, (h, d), dtype=jnp.float32)
        w2 = jax.random.normal(k3, (h, d), dtype=jnp.float32)
        w3 = jax.random.normal(k4, (d, h), dtype=jnp.float32)
        return {'x': x, 'w1': w1, 'w2': w2, 'w3': w3}
    _L0_ffn_all = _L0_ffn_setup()
    _L0_ffn_in = {k: v for k, v in _L0_ffn_all.items() if k in ('w1', 'w2', 'w3')}
    del _L0_ffn_all
    return {'x': x, 'L0_attn_Wq': _L0_attn_in['Wq'], 'L0_attn_Wk': _L0_attn_in['Wk'], 'L0_attn_Wv': _L0_attn_in['Wv'], 'L0_attn_Wo': _L0_attn_in['Wo'], 'L0_attn_qn_w': _L0_attn_in['qn_w'], 'L0_attn_kn_w': _L0_attn_in['kn_w'], 'L0_ffn_w1': _L0_ffn_in['w1'], 'L0_ffn_w2': _L0_ffn_in['w2'], 'L0_ffn_w3': _L0_ffn_in['w3']}

def reference(x, L0_attn_Wq, L0_attn_Wk, L0_attn_Wv, L0_attn_Wo, L0_attn_qn_w, L0_attn_kn_w, L0_ffn_w1, L0_ffn_w2, L0_ffn_w3):
    import jax
    import jax.numpy as jnp

    def _L0_tok_ref(qkv):
        import jax, jax.numpy as jnp
        import numpy as np
        ch = qkv.shape[1] // 3
        q, k, v = jnp.split(qkv, 3, axis=1)
        scale = 1.0 / np.sqrt(np.sqrt(ch)).astype(np.float32)
        weight = jnp.einsum('bct,bcs->bts', q * scale, k * scale)
        weight = jax.nn.softmax(weight.astype(jnp.float32), axis=-1).astype(weight.dtype)
        return jnp.einsum('bts,bcs->bct', weight, v)

    def _L0_attn_ref(x, Wq, Wk, Wv, Wo, qn_w, kn_w):
        import jax, jax.numpy as jnp
        import numpy as np
        HEADS, KV_HEADS, HEAD_DIM = (16, 4, 128)
        WINDOW, ROPE_THETA, EPS = (128, 10000.0, 1e-06)

        def _rms_norm(x, w):
            xf = x.astype(jnp.float32)
            y = xf * jax.lax.rsqrt(jnp.mean(xf * xf, axis=-1, keepdims=True) + EPS)
            return (y * (1.0 + w.astype(jnp.float32))).astype(x.dtype)

        def _rope_cos_sin(T, dtype):
            inv_freq = 1.0 / ROPE_THETA ** (jnp.arange(0, HEAD_DIM, 2, dtype=jnp.float32) / HEAD_DIM)
            pos = jnp.arange(T, dtype=jnp.float32)
            freqs = pos[:, None] * inv_freq[None, :]
            emb = jnp.concatenate([freqs, freqs], axis=-1)
            return (emb.astype(dtype), emb)

        def _rotate_half(x):
            x1, x2 = jnp.split(x, 2, axis=-1)
            return jnp.concatenate([-x2, x1], axis=-1)
        B, T, D = x.shape
        H, Hkv, Dh = (HEADS, KV_HEADS, HEAD_DIM)
        G = H // Hkv
        q = (x @ Wq.T).reshape(B, T, H, Dh).transpose(0, 2, 1, 3)
        k = (x @ Wk.T).reshape(B, T, Hkv, Dh).transpose(0, 2, 1, 3)
        v = (x @ Wv.T).reshape(B, T, Hkv, Dh).transpose(0, 2, 1, 3)
        q = _rms_norm(q, qn_w)
        k = _rms_norm(k, kn_w)
        emb_c, emb_f = _rope_cos_sin(T, x.dtype)
        cos = jnp.cos(emb_f).astype(x.dtype)[None, None]
        sin = jnp.sin(emb_f).astype(x.dtype)[None, None]
        q = q * cos + _rotate_half(q) * sin
        k = k * cos + _rotate_half(k) * sin
        q = q * Dh ** (-0.5)
        qg = q.reshape(B, Hkv, G, T, Dh)
        scores = jnp.einsum('bhgtd,bhkd->bhgtk', qg.astype(jnp.float32), k.astype(jnp.float32))
        dist = jnp.arange(T)[:, None] - jnp.arange(T)[None, :]
        mask = (dist >= 0) & (dist <= WINDOW)
        scores = jnp.where(mask[None, None, None], scores, jnp.finfo(jnp.float32).min)
        att = jax.nn.softmax(scores, axis=-1).astype(x.dtype)
        ctx = jnp.einsum('bhgtk,bhkd->bhgtd', att, v)
        out = ctx.reshape(B, H, T, Dh).transpose(0, 2, 1, 3).reshape(B, T, H * Dh)
        return out @ Wo.T

    def _L0_ffn_ref(x, w1, w2, w3):
        import jax, jax.numpy as jnp
        import numpy as np
        EPS = 1e-08

        def _quantize(w):
            gamma = jnp.mean(jnp.abs(w))
            return jnp.clip(jnp.round(w / (gamma + EPS)), -1.0, 1.0)

        def _bitlinear(x, w):
            return jnp.matmul(x, _quantize(w).T)
        x1 = _bitlinear(x, w1)
        x2 = _bitlinear(x, w2)
        hidden = jax.nn.sigmoid(x1) * x2
        return _bitlinear(hidden, w3)
    h = _L0_tok_ref(x)
    h = h + _L0_attn_ref(_layernorm(h, axis=-1), L0_attn_Wq, L0_attn_Wk, L0_attn_Wv, L0_attn_Wo, L0_attn_qn_w, L0_attn_kn_w)
    h = h + _L0_ffn_ref(_layernorm(h, axis=-1), L0_ffn_w1, L0_ffn_w2, L0_ffn_w3)
    return h

_drawn_inputs = setup_inputs


def setup_inputs(seed=0):
    import zlib

    import numpy as np

    out = dict(_drawn_inputs(seed))
    spreads = {}
    factors = {}
    for name, (base, spread) in spreads.items():
        noise = np.random.default_rng([zlib.crc32(name.encode()), seed]).standard_normal(out[name].shape)
        drawn = base * np.exp(spread * noise) if base else spread * noise
        out[name] = jnp.asarray(drawn.astype(out[name].dtype))
    for name, factor in factors.items():
        out[name] = (out[name] * factor).astype(out[name].dtype)
    return out
```

```python
import numpy as np
import concourse.bass as bass
from concourse import mybir
from contextlib import ExitStack

FP32 = mybir.dt.float32
F32R = mybir.dt.float32r
F16 = mybir.dt.float16
I32 = mybir.dt.int32
ALU = mybir.AluOpType
ACT = mybir.ActivationFunctionType
AX = mybir.AxisListType
MAX_OP = bass.bass_isa.ReduceOp.max
ADD_OP = bass.bass_isa.ReduceOp.add

B, CH, T = 64, 32, 512
P = 128
GB = P // CH
NG = B // GB
NT = T // P
STEPS = GB * NT
DMA = 16
START = 1
TOK_SCALE = float(np.float32(1.0 / np.sqrt(np.sqrt(32.0)))) ** 2


def token_attention(nc, x, vt, h1, ident_in):
    with ExitStack() as ctx:
        def sb(name, shape, dt=FP32):
            return ctx.enter_context(nc.sbuf_tensor(name, shape, dt))

        def pb(name):
            return ctx.enter_context(nc.psum_tensor(name, [P, T], FP32))

        def sem(name):
            return ctx.enter_context(nc.semaphore(name))

        NB = 3
        QP = [sb(f"q_parts{n}", [P, GB, T], F32R) for n in range(NB)]
        KP = [sb(f"k_parts{n}", [P, GB, T], F32R) for n in range(NB)]
        VT = [sb(f"v_t{n}", [P, NT, P]) for n in range(NB)]
        q_raw = sb("q_raw", [P, GB, T])
        k_raw = sb("k_raw", [P, GB, T])
        NE = 3 * GB
        E = sb("exps", [P, NE, T])
        ident = sb("tok_ident", [P, P])
        ones = sb("tok_ones", [P, CH])
        row_max = sb("row_max", [P, STEPS])
        max_parts = sb("max_parts", [P, 2, STEPS], F32R)
        max_t = sb("max_t", [2 * STEPS, P])
        rden = sb("tok_rden", [P, T])
        h_tile = sb("h_tile", [P, T])
        den = sb("tok_den_sum", [P, T])
        out = sb("tok_out_sum", [P, T])

        S = [pb(f"score_rows{n}") for n in range(2)]
        ST = [pb(f"score_cols{n}") for n in range(3)]
        OUT = pb("tok_out")
        DEN = pb("tok_den")
        MT = pb("max_transposed")

        ident_in_sem = sem("t_ident_in")
        const_set = sem("t_const_set")
        q_in, k_in = sem("t_q_in"), sem("t_k_in")
        v_in = [sem(f"t_v_in{n}") for n in range(NB)]
        hi_done, q_lo, k_lo = sem("t_hi_done"), sem("t_q_lo"), sem("t_k_lo")
        s_done, max_done, max_split = sem("t_s_done"), sem("t_max_done"), sem("t_max_split")
        mt_done, mt_out, max_in = sem("t_mt_done"), sem("t_mt_out"), sem("t_max_in")
        st_done, exp_done, pv_done = sem("t_st_done"), sem("t_exp_done"), sem("t_pv_done")
        sums_out, rden_done, h_done, h_out = sem("t_sums_out"), sem("t_rden_done"), sem("t_h_done"), sem("t_h_out")
        EXP_CREDIT = 3
        PV_CREDIT = 3

        AHEAD = 6
        MAX_AT = 2 + STEPS - AHEAD
        FINISHED = 4
        VALUES_AT = [6, 8, 9, 11, 12, 14, 16, 17]
        SPLIT_AT = [2, 4, 6, 8]
        PEEL = NG - 4
        block = ctx.enter_context(nc.Block())

        def over_groups(eng, body):
            with eng.Fori(0, PEEL // NB) as j:
                for p in range(NB):
                    body(j * NB + p, p, True, True)
            for g in range(PEEL, NG):
                body(g, g % NB, g + 1 < NG, g + 2 < NG)

        @block.sync
        def _(sp):
            def load_qk(g):
                for raw, lo, done, first in ((q_raw, q_lo, q_in, 0), (k_raw, k_lo, k_in, CH)):
                    sp.wait_ge(lo, g)
                    for r in range(3):
                        sp.dma_start(raw[r * CH:(r + 1) * CH, :, :],
                                     x[bass.ds(g * GB, GB), first:first + CH, :].rearrange("b c t -> c b t")
                                     ).then_inc(done, DMA)

            def load_v(g, p):
                sp.dma_start(VT[p][:, :, :], vt[bass.ds(g, 1), :, :].rearrange("g s n -> (g s) n")
                             ).then_inc(v_in[p], DMA)

            def store_max(g, p):
                sp.wait_ge(mt_out, g + 1)
                for part in range(2):
                    row = QP[p][3 * CH + part:3 * CH + part + 1, :, :].bitcast(FP32)
                    sp.dma_start(row,
                                 max_t[part * STEPS:(part + 1) * STEPS, :]).then_inc(max_in, DMA)

            sp.dma_start(ident[:, :], ident_in).then_inc(ident_in_sem, DMA)
            load_qk(0)
            load_v(0, 0)
            load_qk(1)
            load_v(1, 1)
            load_qk(2)
            store_max(0, 0)

            def body(g, p, more, more2):
                if more2:
                    sp.wait_ge(pv_done, NT * g + PV_CREDIT)
                    load_v(g + 2, (p + 2) % NB)
                if more:
                    store_max(g + 1, (p + 1) % NB)
                if more2 and not (isinstance(g, int) and g + 3 >= NG):
                    load_qk(g + 3)
                sp.wait_ge(h_done, g + 1 + START)
                sp.dma_start(h1[bass.ds(g * P, P), :], h_tile[:, :]).then_inc(h_out, DMA)

            over_groups(sp, body)
            sp.wait_ge(h_out, NG * DMA + START)

        @block.gpsimd
        def _(pool):
            def split_lo(g, p):
                pool.wait_ge(hi_done, 4 * g + 2)
                nc.gpsimd.tensor_tensor(QP[p][CH:2 * CH, :, :], q_raw[CH:2 * CH, :, :],
                                        QP[p][CH:2 * CH, :, :].bitcast(FP32), ALU.subtract).then_inc(q_lo, 1)
                pool.wait_ge(hi_done, 4 * g + 4)
                nc.gpsimd.tensor_tensor(KP[p][2 * CH:3 * CH, :, :], k_raw[2 * CH:3 * CH, :, :],
                                        KP[p][2 * CH:3 * CH, :, :].bitcast(FP32), ALU.subtract).then_inc(k_lo, 1)

            split_lo(0, 0)
            split_lo(1, 1)

            def body(g, p, more, more2):
                if more2:
                    split_lo(g + 2, (p + 2) % NB)

            over_groups(pool, body)

        @block.scalar
        def _(act):
            def split_hi(g, p, n):
                raw, parts, done = ((q_raw, QP[p], q_in), (k_raw, KP[p], k_in))[n // 2]
                two = slice(2 * (n % 2), 2 * (n % 2) + 2)
                if n % 2 == 0:
                    act.wait_ge(done, 3 * DMA * (g + 1))
                nc.scalar.copy(parts[0:3 * CH, two, :], raw[0:3 * CH, two, :]).then_inc(hi_done, 1)

            for g in range(2):
                for n in range(4):
                    split_hi(g, g, n)

            def exps(g, p, u):
                act.wait_ge(st_done, STEPS * g + u + 1)
                if u % GB == 0:
                    act.wait_ge(pv_done, NT * g + u // GB - 2 + PV_CREDIT)
                nc.scalar.activation(E[:, (STEPS * p + u) % NE, :], ST[(p + u) % 3][:, :], ACT.Exp,
                                     scale=TOK_SCALE).then_inc(exp_done, 1)

            act.sem_inc(sums_out, START)
            act.wait_ge(pv_done, PV_CREDIT)
            exps(0, 0, 0)
            exps(0, 0, 1)

            def body(g, p, more, more2):
                for u in range(2, STEPS + 2):
                    if more2 and u in SPLIT_AT:
                        split_hi(g + 2, (p + 2) % NB, SPLIT_AT.index(u))
                    if u < STEPS:
                        exps(g, p, u)
                    elif more:
                        exps(g + 1, (p + 1) % NB, u - STEPS)
                act.wait_ge(pv_done, NT * (g + 1) + PV_CREDIT)
                act.wait_ge(h_done, g + START)
                nc.scalar.copy(den[:, :], DEN[:, :]).then_inc(sums_out, 1)
                nc.scalar.copy(out[:, :], OUT[:, :]).then_inc(sums_out, 1)

            over_groups(act, body)

        @block.vector
        def _(dve):
            def maximum(g, k):
                dve.wait_ge(s_done, STEPS * g + k + 1)
                nc.vector.reduce_max(row_max[:, k:k + 1], S[k % 2][:, :], AX.X).then_inc(max_done, 1)

            def split_maxima(g):
                dve.wait_ge(max_done, STEPS * (g + 1))
                nc.vector.tensor_scalar(max_parts[:, 0, :], row_max[:, :], -1.0, None, ALU.mult
                                        ).then_inc(max_split, 1)
                dve.wait_ge(max_split, 2 * g + 1)
                nc.vector.scalar_tensor_tensor(max_parts[:, 1, :], row_max[:, :], -1.0,
                                               max_parts[:, 0, :].bitcast(FP32), ALU.mult, ALU.subtract
                                               ).then_inc(max_split, 1)

            def take_transposed(g):
                dve.wait_ge(mt_done, g + 1)
                dve.wait_ge(max_in, 2 * DMA * g)
                nc.vector.tensor_copy(max_t[:, :], MT[0:2 * STEPS, 0:P]).then_inc(mt_out, 1)

            nc.vector.memset(ones[:, :], 1.0).then_inc(const_set, 1)
            for n in range(NB):
                nc.vector.memset(KP[n][3 * CH:3 * CH + 2, :, :].bitcast(FP32), 1.0).then_inc(const_set, 1)
            dve.sem_inc(h_done, START)
            dve.sem_inc(h_out, START)
            for k in range(STEPS):
                maximum(0, k)
            split_maxima(0)
            take_transposed(0)
            EARLY = AHEAD + 2 * FINISHED
            for k in range(EARLY):
                maximum(1, k)

            def body(g, p, more, more2):
                if more:
                    for k in range(EARLY, STEPS):
                        maximum(g + 1, k)
                    split_maxima(g + 1)
                    take_transposed(g + 1)
                    if more2:
                        for k in range(AHEAD):
                            maximum(g + 2, k)
                dve.wait_ge(sums_out, 2 * g + 1 + START)
                for n in range(FINISHED):
                    part = slice(n * T // FINISHED, (n + 1) * T // FINISHED)
                    nc.vector.reciprocal(rden[:, part], den[:, part]).then_inc(rden_done, 1)
                    if more2:
                        maximum(g + 2, AHEAD + 2 * n)
                        maximum(g + 2, AHEAD + 2 * n + 1)
                dve.wait_ge(rden_done, FINISHED * (g + 1))
                dve.wait_ge(sums_out, 2 * g + 2 + START)
                dve.wait_ge(h_out, DMA * g + START)
                nc.vector.tensor_tensor(h_tile[:, :], out[:, :], rden[:, :], ALU.mult).then_inc(h_done, 1)

            over_groups(dve, body)

        @block.tensor
        def _(pe):
            def rows(g, p, k):
                b, t = k // NT, k % NT
                if k == 0:
                    pe.wait_ge(q_lo, g + 1)
                    pe.wait_ge(k_lo, g + 1)
                if not (isinstance(g, int) and STEPS * g + k < 2):
                    pe.wait_ge(max_done, STEPS * g + k - 1)
                nc.tensor.matmul(S[k % 2][:, :], QP[p][0:3 * CH, b, t * P:(t + 1) * P], KP[p][0:3 * CH, b, :],
                                 start=True, stop=True).then_inc(s_done, 1)

            def transpose_maxima(g):
                pe.wait_ge(max_split, 2 * (g + 1))
                pe.wait_ge(mt_out, g)
                nc.tensor.matmul(MT[0:2 * STEPS, 0:P], max_parts[:, :, :].bitcast(FP32), ident[:, :],
                                 start=True, stop=True).then_inc(mt_done, 1)

            def cols(g, p, u):
                i, b = u // GB, u % GB
                if u == 0:
                    pe.wait_ge(max_in, 2 * DMA * (g + 1))
                pe.wait_ge(exp_done, STEPS * g + u - 2 + EXP_CREDIT)
                nc.tensor.matmul(ST[(p + u) % 3][:, :], KP[p][0:3 * CH + 2, b, i * P:(i + 1) * P],
                                 QP[p][0:3 * CH + 2, b, :], start=True, stop=True).then_inc(st_done, 1)

            def values(g, p, i, sums):
                if i == 0 and not sums:
                    pe.wait_ge(sums_out, 2 * g + START)
                    pe.wait_ge(v_in[p], g_over(g, p))
                pe.wait_ge(exp_done, STEPS * g + GB * (i + 1) + EXP_CREDIT)
                for b in range(GB):
                    into, by = (DEN, ones[:, :]) if sums else (OUT, VT[p][:, i, b * CH:(b + 1) * CH])
                    last = nc.tensor.matmul(into[b * CH:(b + 1) * CH, :], by, E[:, (STEPS * p + GB * i + b) % NE, :],
                                            start=(i == 0), stop=(i == NT - 1))
                if sums:
                    last.then_inc(pv_done, 1)

            turns = {}

            def g_over(g, p):
                if isinstance(g, int):
                    return DMA * (g // NB + 1)
                return DMA * (turns["j"] + 1)

            pe.wait_ge(ident_in_sem, DMA)
            pe.wait_ge(const_set, 1 + NB)
            for _ in range(EXP_CREDIT):
                pe.sem_inc(exp_done, 1)
            for _ in range(PV_CREDIT):
                pe.sem_inc(pv_done, 1)
            for k in range(STEPS):
                rows(0, 0, k)
            transpose_maxima(0)
            cols(0, 0, 0)
            cols(0, 0, 1)
            for k in range(AHEAD):
                rows(1, 1, k)

            def body(g, p, more, more2):
                q = (p + 1) % NB
                for u in range(2, STEPS + 2):
                    if more and u == MAX_AT:
                        transpose_maxima(g + 1)
                    if u < MAX_AT and more:
                        rows(g + 1, q, u - 2 + AHEAD)
                    if u >= MAX_AT and more2:
                        rows(g + 2, (p + 2) % NB, u - MAX_AT)
                    if u < STEPS:
                        cols(g, p, u)
                    elif more:
                        cols(g + 1, q, u - STEPS)
                    if u in VALUES_AT:
                        values(g, p, *divmod(VALUES_AT.index(u), 2))

            with pe.Fori(0, PEEL // NB) as j:
                turns["j"] = j
                for p in range(NB):
                    body(j * NB + p, p, True, True)
            for g in range(PEEL, NG):
                body(g, g % NB, g + 1 < NG, g + 2 < NG)


D = 512
KD = D // P
TOK = 64 * 32
NTT = TOK // P
SEQ = 32
BT = P // SEQ
HEADS, KV, HD = 16, 4, 128
G = HEADS // KV
FF = 1408
KF = FF // P
QKV_W = KD * (HEADS + 2 * KV) * HD
Q_AT, K_AT, V_AT, O_AT = 0, KD * HEADS * HD, KD * (HEADS + KV) * HD, QKV_W
ATTN_W = QKV_W + HEADS * D
FFN_W = 3 * KD * FF
X_SCALE = 2.0 ** 11
V_SHIFT = 2.0 ** -16
LN_EPS, RMS_EPS, GAMMA_EPS = 1e-5, 1e-6, 1e-8
A_CHUNK, F_CHUNK = 1024, FF
A_CHUNKS, F_CHUNKS = ATTN_W // A_CHUNK, FFN_W // F_CHUNK
ATTN_PARTS = ((Q_AT, K_AT), (K_AT, V_AT), (V_AT, O_AT), (O_AT, ATTN_W))


def weights(nc, W, w_attn, w_ffn):
    with ExitStack() as ctx:
        def sb(name, shape, dt=FP32):
            return ctx.enter_context(nc.sbuf_tensor(name, shape, dt))

        def sem(name):
            return ctx.enter_context(nc.semaphore(name))

        RING = 2
        raw_a = [sb(f"raw_attn{n}", [P, A_CHUNK]) for n in range(RING)]
        raw_f = [sb(f"raw_ffn{n}", [P, F_CHUNK]) for n in range(RING)]
        below = sb("w_below", [P, F_CHUNK], F16)
        amax = sb("w_amax", [P, A_CHUNKS])
        fsum = sb("w_fsum", [P, F_CHUNKS])
        amax4 = sb("w_amax4", [P, 4])
        fsum3 = sb("w_fsum3", [P, 3])
        amax_all = sb("w_amax_all", [P, 4])
        fsum_all = sb("w_fsum_all", [P, 3])
        thr = sb("w_thr", [P, 3])
        nthr = sb("w_nthr", [P, 3])
        tmp = sb("w_tmp", [P, 4])
        pow2 = sb("w_pow2", [P, 4])

        a_in = [sem(f"w_a_in{n}") for n in range(RING)]
        f_in = [sem(f"w_f_in{n}") for n in range(RING)]
        a_stat, f_stat = sem("w_a_stat"), sem("w_f_stat")
        folded, reduced, chain = sem("w_folded"), sem("w_reduced"), sem("w_chain")
        a_hi, a_lo, f_done = sem("w_a_hi"), sem("w_a_lo"), sem("w_f_done")
        block = ctx.enter_context(nc.Block())

        @block.sync
        def _(sp):
            for again, (a_free, f_free) in enumerate(((a_stat, f_stat), (a_lo, f_done))):
                with sp.Fori(0, A_CHUNKS // RING) as j:
                    for n in range(RING):
                        if again:
                            sp.wait_ge(a_stat, A_CHUNKS + START)
                        sp.wait_ge(a_free, j * RING + START)
                        sp.dma_start(raw_a[n][:, :], w_attn[:, bass.ds((j * RING + n) * A_CHUNK, A_CHUNK)]
                                     ).then_inc(a_in[n], DMA)
                with sp.Fori(0, F_CHUNKS // RING) as j:
                    for n in range(RING):
                        if again:
                            sp.wait_ge(f_stat, F_CHUNKS + START)
                        sp.wait_ge(f_free, j * RING + START)
                        sp.dma_start(raw_f[n][:, :], w_ffn[:, bass.ds((j * RING + n) * F_CHUNK, F_CHUNK)]
                                     ).then_inc(f_in[n], DMA)

        @block.gpsimd
        def _(pool):
            pool.wait_ge(folded, 7)
            nc.gpsimd.partition_all_reduce(amax_all[:, :], amax4[:, :], P, MAX_OP
                                           ).then_inc(reduced, 1)
            pool.wait_ge(reduced, 1)
            nc.gpsimd.partition_all_reduce(fsum_all[:, :], fsum3[:, :], P, ADD_OP).then_inc(reduced, 1)

        @block.vector
        def _(dve):
            for start in (a_stat, f_stat, a_lo, f_done):
                dve.sem_inc(start, START)
            with dve.Fori(0, A_CHUNKS // RING) as j:
                for n in range(RING):
                    dve.wait_ge(a_in[n], DMA * (j + 1))
                    nc.vector.tensor_reduce(amax[:, bass.ds(j * RING + n, 1)], raw_a[n][:, :], AX.X, ALU.max,
                                            apply_absolute_value=True).then_inc(a_stat, 1)
            with dve.Fori(0, F_CHUNKS // RING) as j:
                for n in range(RING):
                    dve.wait_ge(f_in[n], DMA * (j + 1))
                    nc.vector.tensor_reduce(fsum[:, bass.ds(j * RING + n, 1)], raw_f[n][:, :], AX.X, ALU.add,
                                            apply_absolute_value=True).then_inc(f_stat, 1)
            dve.wait_ge(a_stat, A_CHUNKS + START)
            dve.wait_ge(f_stat, F_CHUNKS + START)
            for m, (lo, hi) in enumerate(ATTN_PARTS):
                nc.vector.tensor_reduce(amax4[:, m:m + 1], amax[:, lo // A_CHUNK:hi // A_CHUNK], AX.X, ALU.max
                                        ).then_inc(folded, 1)
            for m in range(3):
                nc.vector.tensor_reduce(fsum3[:, m:m + 1], fsum[:, m * KD:(m + 1) * KD], AX.X, ALU.add
                                        ).then_inc(folded, 1)
            steps = [0]

            def link(ins):
                steps[0] += 1
                ins.then_inc(chain, 1)
                dve.wait_ge(chain, steps[0])

            dve.wait_ge(reduced, 2)
            link(nc.vector.tensor_scalar(tmp[:, :], amax_all[:, :], 1e-30, None, ALU.max))
            link(nc.vector.tensor_scalar(pow2[:, :].bitcast(I32), tmp[:, :].bitcast(I32), 0x7f800000, None,
                                         ALU.bitwise_and))
            link(nc.vector.reciprocal(tmp[:, :], pow2[:, :]))
            link(nc.vector.tensor_scalar(W.scale[:, :], tmp[:, :], 2.0 ** 10, None, ALU.mult))
            link(nc.vector.tensor_tensor(tmp[:, :], W.scale[:, :], W.scale[:, :], ALU.mult))
            link(nc.vector.tensor_scalar(W.eps_q[:, :], tmp[:, 0:1], HD * RMS_EPS * X_SCALE ** 2, None, ALU.mult))
            link(nc.vector.tensor_scalar(W.eps_k[:, :], tmp[:, 1:2], RMS_EPS * X_SCALE ** 2, None, ALU.mult))
            link(nc.vector.tensor_tensor(tmp[:, 0:1], pow2[:, 2:3], pow2[:, 3:4], ALU.mult))
            link(nc.vector.tensor_scalar(W.o_unscale[:, :], tmp[:, 0:1], 2.0 ** -15, None, ALU.mult))
            link(nc.vector.tensor_scalar(tmp[:, 0:3], fsum_all[:, :], 1.0 / (FF * D), GAMMA_EPS, ALU.mult, ALU.add))
            link(nc.vector.tensor_scalar(thr[:, :], tmp[:, 0:3], 0.5, None, ALU.mult))
            link(nc.vector.tensor_scalar(nthr[:, :], tmp[:, 0:3], -0.5, None, ALU.mult))
            for m, (lo, hi) in enumerate(ATTN_PARTS):
                with dve.Fori(lo // A_CHUNK // RING, hi // A_CHUNK // RING) as j:
                    for n in range(RING):
                        c = j * RING + n
                        dve.wait_ge(a_hi, c + 1)
                        nc.vector.scalar_tensor_tensor(W.a_lo[:, bass.ds(c * A_CHUNK, A_CHUNK)], raw_a[n][:, :],
                                                       W.scale[:, m:m + 1], W.a_hi[:, bass.ds(c * A_CHUNK, A_CHUNK)],
                                                       ALU.mult, ALU.subtract).then_inc(a_lo, 1)
            for m in range(3):
                with dve.Fori(m * KD // RING, (m + 1) * KD // RING) as j:
                    for n in range(RING):
                        c = j * RING + n
                        dve.wait_ge(f_in[n], DMA * (j + 1 + F_CHUNKS // RING))
                        nc.vector.tensor_scalar(below[:, :], raw_f[n][:, :], nthr[:, m:m + 1], None, ALU.is_lt
                                                ).then_inc(f_stat, 1)
                        dve.wait_ge(f_stat, F_CHUNKS + c + 1 + START)
                        nc.vector.scalar_tensor_tensor(W.ffn[:, bass.ds(c * F_CHUNK, F_CHUNK)], raw_f[n][:, :],
                                                       thr[:, m:m + 1], below[:, :], ALU.is_gt, ALU.subtract
                                                       ).then_inc(f_done, 1)
                        dve.wait_ge(f_done, c + 1 + START)

        @block.scalar
        def _(act):
            act.wait_ge(chain, 4)
            for m, (lo, hi) in enumerate(ATTN_PARTS):
                with act.Fori(lo // A_CHUNK // RING, hi // A_CHUNK // RING) as j:
                    for n in range(RING):
                        c = j * RING + n
                        act.wait_ge(a_in[n], DMA * (j + 1 + A_CHUNKS // RING))
                        nc.scalar.activation(W.a_hi[:, bass.ds(c * A_CHUNK, A_CHUNK)], raw_a[n][:, :], ACT.Copy,
                                             scale=W.scale[:, m:m + 1]).then_inc(a_hi, 1)


def blocks(nc, W, h1, tables_in, norm_in, mask_in, block_in, ident_in, out):
    with ExitStack() as ctx:
        def sb(name, shape, dt=FP32):
            return ctx.enter_context(nc.sbuf_tensor(name, shape, dt))

        def sem(name):
            return ctx.enter_context(nc.semaphore(name))

        PROJ = [ctx.enter_context(nc.psum_tensor(f"proj{n}", [P, D], FP32)) for n in range(2)]
        TR = [ctx.enter_context(nc.psum_tensor(f"transposed{n}", [P, D], FP32)) for n in range(2)]
        FB = [ctx.enter_context(nc.psum_tensor(f"ffn_sum{n}", [P, D], FP32)) for n in range(4)]
        PV_BANK = [FB[0], FB[1], FB[3], FB[0]]
        SCORES = FB[2]

        tables = sb("tables", [P, 4, HD])
        norm_w = sb("norm_w", [P, 4, HD])
        mask = sb("mask", [P, SEQ])
        own = sb("own_batch", [P, BT])
        ident = sb("ident", [P, P])
        minus_half = sb("minus_half", [P, HEADS])
        h_ln = sb("h_ln", [P, D])
        h_res = sb("h_res", [P, D])
        stats = sb("stats", [P, 2, 6])
        mv = sb("mv", [P, 2, 2])
        var = sb("var", [P, 2, 1])
        rstd = sb("rstd", [P, 2, 1])
        xn = sb("xn", [P, D])
        xh, xl = sb("x_hi", [P, D], F16), sb("x_lo", [P, D], F16)
        sq = [sb(f"squares{n}", [P, D]) for n in range(2)]
        ss = sb("sums_sq", [P, KV + HEADS])
        ms = sb("mean_sq", [P, KV + HEADS])
        rr = sb("rms_inv", [P, KV + HEADS])
        ra = [sb(f"rope_cos{n}", [P, D]) for n in range(2)]
        rb = [sb(f"rope_sin{n}", [P, D]) for n in range(2)]
        rope = sb("roped", [P, 1 + KV, D])
        kT = sb("k_t", [P, KV, P])
        qT = sb("q_t", [P, KV, G * P])
        v = sb("v", [P, KV * HD])
        sm = sb("scores", [P, HEADS, SEQ])
        sd = sb("scores_less_max", [P, HEADS, SEQ])
        pr = sb("probs", [P, HEADS, SEQ])
        mx = sb("row_maxima", [P, HEADS])
        den = sb("row_sums", [P, HEADS])
        rden = sb("row_sums_inv", [P, HEADS])
        pbd = sb("probs_blocks", [P, KV, BT, G * SEQ])
        ch, cl = sb("ctx_hi", [P, HEADS, P], F16), sb("ctx_lo", [P, HEADS, P], F16)
        h2 = sb("h2", [P, D])
        x2n = sb("x2n", [P, D])
        x2h, x2l = sb("x2_hi", [P, D], F16), sb("x2_lo", [P, D], F16)
        th = sb("tanh", [P, D])
        hid = sb("hidden", [P, D])
        hh, hl = sb("hidden_hi", [P, KF, P], F16), sb("hidden_lo", [P, KF, P], F16)
        o_tile = sb("out_tile", [P, D])

        const_in, const_set = sem("b_const_in"), sem("b_const_set")
        ln_in, res_in, out_done = sem("b_ln_in"), sem("b_res_in"), sem("b_out_done")
        ln1_var, ln1_rstd, ln1 = sem("b_ln1_var"), sem("b_ln1_rstd"), sem("b_ln1")
        ln2_var, ln2_rstd, ln2 = sem("b_ln2_var"), sem("b_ln2_rstd"), sem("b_ln2")
        xt, x_hi, x_lo = sem("b_xt"), sem("b_x_hi"), sem("b_x_lo")
        proj, squared, ssum, roped_a, roped_b = (sem("b_proj"), sem("b_squared"), sem("b_ssum"), sem("b_roped_a"),
                                                 sem("b_roped_b"))
        added, mean_sq, rms, q_ready, v_out = (sem("b_added"), sem("b_mean_sq"), sem("b_rms"), sem("b_q_ready"),
                                               sem("b_v_out"))
        qkt, qkt_out = sem("b_qkt"), sem("b_qkt_out")
        scored, masked, sub, exped, probs = (sem("b_scored"), sem("b_masked"), sem("b_sub"), sem("b_exped"),
                                             sem("b_probs"))
        soft = sem("b_soft")
        ln1_self, ln2_self = sem("b_ln1_self"), sem("b_ln2_self")
        pt, pbd_out, pv, c_hi, c_lo = sem("b_pt"), sem("b_pbd_out"), sem("b_pv"), sem("b_c_hi"), sem("b_c_lo")
        o_sum, h2_done = sem("b_o_sum"), sem("b_h2_done")
        xt2, x2_hi, x2_lo = sem("b_xt2"), sem("b_x2_hi"), sem("b_x2_lo")
        f1, tanhed, gated, hid_hi, hid_lo = (sem("b_f1"), sem("b_tanhed"), sem("b_gated"), sem("b_hid_hi"),
                                             sem("b_hid_lo"))
        w3, o_out = sem("b_w3"), sem("b_o_out")

        NPROJ = 2 + KV
        FG = [range(0, 4), range(4, 8), range(8, KF)]
        NF = len(FG)
        block = ctx.enter_context(nc.Block())

        def over_tiles(eng, body):
            body(0, True, False)
            with eng.Fori(1, NTT - 1) as n:
                body(n, True, True)
            body(NTT - 1, True, True)
            body(NTT, False, True)

        def bcast(ap, shape, at):
            return ap.unsqueeze(at).to_broadcast(shape)

        @block.sync
        def _(sp):
            for dst, src in ((tables[:, :, :], tables_in), (norm_w[:, :, :], norm_in), (mask[:, :], mask_in),
                             (own[:, :], block_in), (ident[:, :], ident_in)):
                sp.dma_start(dst, src).then_inc(const_in, DMA)
            sp.dma_start(h_ln[:, :], h1[0:P, :]).then_inc(ln_in, DMA)

            def body(n, attn, ffn):
                if attn and not (isinstance(n, int) and n + 1 >= NTT):
                    sp.wait_ge(ln1, n + 1)
                    sp.dma_start(h_ln[:, :], h1[bass.ds((n + 1) * P, P), :]).then_inc(ln_in, DMA)
                if attn:
                    sp.wait_ge(h2_done, n)
                    sp.dma_start(h_res[:, :], h1[bass.ds(n * P, P), :]).then_inc(res_in, DMA)
                if ffn:
                    sp.wait_ge(o_out, n + START)
                    sp.dma_start(out[bass.ds((n - 1) * P, P), :], o_tile[:, :]).then_inc(out_done, DMA)

            over_tiles(sp, body)
            sp.wait_ge(out_done, DMA * NTT + START)

        @block.gpsimd
        def _(pool):
            def inv_std(n, m, var_done, out_sem):
                pool.wait_ge(var_done, n + 1)
                nc.gpsimd.tensor_tensor(rstd[:, m, :], var[:, m, :], minus_half[:, 0:1], ALU.pow).then_inc(out_sem, 1)

            pool.wait_ge(const_set, 2)
            inv_std(0, 0, ln1_var, ln1_rstd)

            def body(n, attn, ffn):
                if not attn:
                    return

                def add_parts(c):
                    pool.wait_ge(roped_b, 5 * n + c + 1)
                    nc.gpsimd.tensor_tensor(rope[:, c, :], ra[c % 2][:, :], rb[c % 2][:, :], ALU.add
                                            ).then_inc(added, 1)

                def invert(lo, hi, k):
                    pool.wait_ge(mean_sq, 2 * n + k + 1)
                    nc.gpsimd.tensor_tensor(rr[:, lo:hi], ms[:, lo:hi], minus_half[:, 0:hi - lo], ALU.pow
                                            ).then_inc(rms, 1)

                def normalise(c):
                    pool.wait_ge(added, 5 * n + c + 1)
                    view = rope[:, c, :].rearrange("p (h d) -> p h d", d=HD)
                    nc.gpsimd.tensor_tensor(view, view, bcast(rr[:, G * c:G * c + G], [P, G, HD], 2), ALU.mult
                                            ).then_inc(q_ready, 1)

                add_parts(0)
                invert(0, KV, 0)
                pool.wait_ge(rms, 2 * n + 1)
                normalise(0)
                for c in range(1, 1 + KV):
                    add_parts(c)
                invert(KV, KV + HEADS, 1)
                pool.wait_ge(rms, 2 * n + 2)
                for c in range(1, 1 + KV):
                    normalise(c)
                inv_std(n + 1, 0, ln1_var, ln1_rstd) if not (isinstance(n, int) and n + 1 >= NTT) else None
                inv_std(n, 1, ln2_var, ln2_rstd)

            over_tiles(pool, body)

        @block.scalar
        def _(act):
            def body(n, attn, ffn):
                if attn:
                    act.wait_ge(xt, n + 1)
                    nc.scalar.copy(xh[:, :], TR[0][:, :]).then_inc(x_hi, 1)
                    for c in range(1 + KV):
                        act.wait_ge(proj, NPROJ * n + c + 1)
                        if not (isinstance(n, int) and 5 * n + c < 2):
                            act.wait_ge(ssum, 5 * n + c - 1)
                        nc.scalar.activation(sq[c % 2][:, :], PROJ[c % 2][:, :], ACT.Square).then_inc(squared, 1)
                    act.wait_ge(proj, NPROJ * (n + 1))
                    nc.scalar.mul(v[:, :], PROJ[1][:, :], V_SHIFT).then_inc(v_out, 1)
                if ffn:
                    act.wait_ge(xt2, n)
                    nc.scalar.copy(x2h[:, :], TR[1][:, :]).then_inc(x2_hi, 1)
                    for f, tiles in enumerate(FG):
                        w = len(tiles) * P
                        act.wait_ge(f1, NF * (n - 1) + f + 1)
                        act.wait_ge(gated, NF * (n - 1) + f + START)
                        nc.scalar.activation(th[:, 0:w], FB[2 * (f % 2)][:, 0:w], ACT.Tanh,
                                             scale=0.5 / X_SCALE).then_inc(tanhed, 1)
                        act.wait_ge(gated, NF * (n - 1) + f + 1 + START)
                        nc.scalar.mul(hh[:, tiles[0]:tiles[-1] + 1, :].rearrange("p k t -> p (k t)"), hid[:, 0:w],
                                      2.0 ** -6).then_inc(hid_hi, 1)
                if attn:
                    for c in range(1 + KV):
                        act.wait_ge(qkt, 5 * n + c + 1)
                        src = TR[c % 2][:, :]
                        if c == 0:
                            nc.scalar.copy(kT[:, :, :].rearrange("p h t -> p (h t)"), src).then_inc(qkt_out, 1)
                        else:
                            nc.scalar.copy(qT[:, c - 1, :].rearrange("p (b g t) -> p g b t", g=G, b=BT),
                                           src.rearrange("p (g b t) -> p g b t", g=G, b=BT)).then_inc(qkt_out, 1)
                    act.wait_ge(sub, n + 1)
                    nc.scalar.activation(pr[:, :, :], sd[:, :, :], ACT.Exp).then_inc(exped, 1)
                    for h in range(KV):
                        act.wait_ge(pv, KV * n + h + 1)
                        nc.scalar.copy(ch[:, G * h:G * h + G, :].rearrange("p g (b t) -> p b g t", b=BT),
                                       PV_BANK[h][:, :].rearrange("p (b g t) -> p b g t", g=G, b=BT)).then_inc(c_hi, 1)

            over_tiles(act, body)

        @block.vector
        def _(dve):
            for start in (o_out, gated, out_done):
                dve.sem_inc(start, START)
            nc.vector.memset(minus_half[:, :], -0.5).then_inc(const_set, 1)
            dve.wait_ge(const_in, 5 * DMA)
            nc.vector.scalar_tensor_tensor(tables[:, :, :], norm_w[:, :, :], 1.0, tables[:, :, :], ALU.add, ALU.mult
                                           ).then_inc(const_set, 1)

            def ln_stats(n, m, src, var_done, self_sem):
                nc.vector.bn_stats(stats[:, m, :], src).then_inc(self_sem, 1)
                dve.wait_ge(self_sem, 3 * n + 1)
                dve.sem_inc(self_sem, 1)
                nc.vector.bn_aggr(mv[:, m, :], stats[:, m, :]).then_inc(self_sem, 1)
                dve.wait_ge(self_sem, 3 * n + 3)
                nc.vector.tensor_scalar(var[:, m, :], mv[:, m, 1:2], LN_EPS, X_SCALE ** -2, ALU.add, ALU.mult
                                        ).then_inc(var_done, 1)

            def ln_apply(n, m, src, dst, rstd_done, done):
                dve.wait_ge(rstd_done, n + 1)
                nc.vector.tensor_scalar(dst, src, mv[:, m, 0:1], rstd[:, m, :], ALU.subtract, ALU.mult
                                        ).then_inc(done, 1)

            dve.wait_ge(const_set, 2)
            dve.wait_ge(ln_in, DMA)
            ln_stats(0, 0, h_ln[:, :], ln1_var, ln1_self)
            ln_apply(0, 0, h_ln[:, :], xn[:, :], ln1_rstd, ln1)

            def body(n, attn, ffn):
                last = isinstance(n, int) and n + 1 >= NTT
                if attn:
                    dve.wait_ge(x_hi, n + 1)
                    nc.vector.tensor_tensor(xl[:, :], TR[0][:, :], xh[:, :], ALU.subtract).then_inc(x_lo, 1)
                    for c in range(1 + KV):
                        dve.wait_ge(squared, 5 * n + c + 1)
                        if not (isinstance(n, int) and 5 * n + c < 2):
                            dve.wait_ge(added, 5 * n + c - 1)
                        w = 2 if c == 0 else 0
                        y = PROJ[c % 2][:, :].rearrange("p (h d) -> p h d", d=HD)
                        a = ra[c % 2][:, :].rearrange("p (h d) -> p h d", d=HD)
                        b = rb[c % 2][:, :].rearrange("p (h d) -> p h d", d=HD)
                        half = HD // 2
                        nc.vector.tensor_tensor(a, y, bcast(tables[:, w, :], [P, G, HD], 1), ALU.mult
                                                ).then_inc(roped_a, 1)
                        nc.vector.tensor_tensor(b[:, :, 0:half], y[:, :, half:HD],
                                                bcast(tables[:, w + 1, 0:half], [P, G, half], 1), ALU.mult
                                                ).then_inc(roped_a, 1)
                        nc.vector.tensor_tensor(b[:, :, half:HD], y[:, :, 0:half],
                                                bcast(tables[:, w + 1, half:HD], [P, G, half], 1), ALU.mult
                                                ).then_inc(roped_b, 1)
                        nc.vector.tensor_reduce(ss[:, G * c:G * c + G],
                                                sq[c % 2][:, :].rearrange("p (h d) -> p h d", d=HD), AX.X, ALU.add
                                                ).then_inc(ssum, 1)
                        if c == 0:
                            dve.wait_ge(ssum, 5 * n + 1)
                            nc.vector.tensor_scalar(ms[:, 0:KV], ss[:, 0:KV], 1.0 / HD, W.eps_k[:, :], ALU.mult,
                                                    ALU.add).then_inc(mean_sq, 1)
                    dve.wait_ge(ssum, 5 * n + 5)
                    nc.vector.tensor_scalar(ms[:, KV:], ss[:, KV:], W.eps_q[:, :], None, ALU.add).then_inc(mean_sq, 1)
                if ffn:
                    dve.wait_ge(x2_hi, n)
                    nc.vector.tensor_tensor(x2l[:, :], TR[1][:, :], x2h[:, :], ALU.subtract).then_inc(x2_lo, 1)
                    for f, tiles in enumerate(FG):
                        w = len(tiles) * P
                        dve.wait_ge(tanhed, NF * (n - 1) + f + 1)
                        nc.vector.scalar_tensor_tensor(hid[:, 0:w], th[:, 0:w], 1.0, FB[2 * (f % 2) + 1][:, 0:w],
                                                       ALU.add, ALU.mult).then_inc(gated, 1)
                        dve.wait_ge(hid_hi, NF * (n - 1) + f + 1)
                        nc.vector.scalar_tensor_tensor(
                            hl[:, tiles[0]:tiles[-1] + 1, :].rearrange("p k t -> p (k t)"), hid[:, 0:w], 2.0 ** -6,
                            hh[:, tiles[0]:tiles[-1] + 1, :].rearrange("p k t -> p (k t)"), ALU.mult, ALU.subtract
                        ).then_inc(hid_lo, 1)
                        dve.wait_ge(hid_lo, NF * (n - 1) + f + 1)
                if attn:
                    step = [0]

                    def link(ins):
                        step[0] += 1
                        ins.then_inc(soft, 1)
                        dve.wait_ge(soft, 4 * n + step[0])

                    dve.wait_ge(scored, n + 1)
                    nc.vector.tensor_tensor(sm[:, :, :], SCORES[:, :].rearrange("p (u k) -> p u k", k=SEQ),
                                            bcast(mask[:, :], [P, HEADS, SEQ], 1), ALU.add).then_inc(masked, 1)
                    dve.wait_ge(masked, n + 1)
                    link(nc.vector.tensor_reduce(mx[:, :], sm[:, :, :], AX.X, ALU.max))
                    nc.vector.tensor_tensor(sd[:, :, :], sm[:, :, :], bcast(mx[:, :], [P, HEADS, SEQ], 2),
                                            ALU.subtract).then_inc(sub, 1)
                    dve.wait_ge(exped, n + 1)
                    link(nc.vector.tensor_reduce(den[:, :], pr[:, :, :], AX.X, ALU.add))
                    link(nc.vector.reciprocal(rden[:, :], den[:, :]))
                    link(nc.vector.tensor_tensor(pr[:, :, :], pr[:, :, :], bcast(rden[:, :], [P, HEADS, SEQ], 2),
                                                 ALU.mult))
                if ffn:
                    dve.wait_ge(w3, n)
                    dve.wait_ge(out_done, DMA * (n - 1) + START)
                    nc.vector.scalar_tensor_tensor(o_tile[:, :], PROJ[0][:, :], 2.0 ** -6, h2[:, :], ALU.mult, ALU.add
                                                   ).then_inc(o_out, 1)
                if attn:
                    dve.wait_ge(pt, n + 1)
                    for h in range(KV):
                        nc.vector.tensor_tensor(pbd[:, h, :, :],
                                                bcast(TR[1][:, h * P:(h + 1) * P], [P, BT, G * SEQ], 1),
                                                bcast(own[:, :], [P, BT, G * SEQ], 2), ALU.mult).then_inc(pbd_out, 1)
                    for h in range(KV):
                        dve.wait_ge(c_hi, KV * n + h + 1)
                        view = dict(g=G, b=BT)
                        nc.vector.tensor_tensor(cl[:, G * h:G * h + G, :].rearrange("p g (b t) -> p b g t", b=BT),
                                                PV_BANK[h][:, :].rearrange("p (b g t) -> p b g t", **view),
                                                ch[:, G * h:G * h + G, :].rearrange("p g (b t) -> p b g t", b=BT),
                                                ALU.subtract).then_inc(c_lo, 1)
                    if not last:
                        dve.wait_ge(ln_in, DMA * (n + 2))
                        ln_stats(n + 1, 0, h_ln[:, :], ln1_var, ln1_self)
                        ln_apply(n + 1, 0, h_ln[:, :], xn[:, :], ln1_rstd, ln1)
                    dve.wait_ge(o_sum, n + 1)
                    dve.wait_ge(res_in, DMA * (n + 1))
                    nc.vector.scalar_tensor_tensor(h2[:, :], PROJ[1][:, :], W.o_unscale[:, :], h_res[:, :], ALU.mult,
                                                   ALU.add).then_inc(h2_done, 1)
                    dve.wait_ge(h2_done, n + 1)
                    ln_stats(n, 1, h2[:, :], ln2_var, ln2_self)
                    ln_apply(n, 1, h2[:, :], x2n[:, :], ln2_rstd, ln2)

            over_tiles(dve, body)

        @block.tensor
        def _(pe):
            pe.wait_ge(const_in, 5 * DMA)

            def transpose(dst, src, last_sem):
                for k in range(KD):
                    t = nc.tensor.transpose(dst[:, k * P:(k + 1) * P], src[:, k * P:(k + 1) * P], ident[:, :])
                t.then_inc(last_sem, 1)

            def split_products(dst, pairs, done):
                for i, (ah, al, bh, bl) in enumerate(pairs):
                    nc.tensor.matmul(dst, ah, bh, start=(i == 0), stop=False)
                    nc.tensor.matmul(dst, ah, bl, start=False, stop=False)
                    t = nc.tensor.matmul(dst, al, bh, start=False, stop=(i == len(pairs) - 1))
                t.then_inc(done, 1)

            def body(n, attn, ffn):
                first = isinstance(n, int) and n == 0
                if attn:
                    pe.wait_ge(ln1, n + 1)
                    pe.wait_ge(qkt_out, 5 * n)
                    transpose(TR[0], xn, xt)
                    pe.wait_ge(x_hi, n + 1)
                    pe.wait_ge(x_lo, n + 1)
                    for c in range(NPROJ):
                        if c == 0 and not first:
                            pe.wait_ge(o_out, n - 1 + START)
                        if c == 1:
                            pe.wait_ge(h2_done, n)
                        if c >= 2:
                            pe.wait_ge(squared, 5 * n + c - 1)
                            pe.wait_ge(roped_b, 5 * n + c - 1)
                        pairs = []
                        for k in range(KD):
                            at = (K_AT + k * KV * HD if c == 0 else V_AT + k * KV * HD if c == NPROJ - 1
                                  else Q_AT + k * HEADS * HD + (c - 1) * D)
                            pairs.append((xh[:, k * P:(k + 1) * P], xl[:, k * P:(k + 1) * P],
                                          W.a_hi[:, at:at + D], W.a_lo[:, at:at + D]))
                        split_products(PROJ[c % 2][:, :], pairs, proj)
                if ffn:
                    pe.wait_ge(ln2, n)
                    pe.wait_ge(pbd_out, KV * n)
                    transpose(TR[1], x2n, xt2)
                    pe.wait_ge(x2_hi, n)
                    pe.wait_ge(x2_lo, n)
                    pe.wait_ge(c_hi, KV * n)
                    pe.wait_ge(c_lo, KV * n)
                    pe.wait_ge(masked, n)
                    for f, tiles in enumerate(FG):
                        if f == 2:
                            pe.wait_ge(tanhed, NF * (n - 1) + 1)
                            pe.wait_ge(gated, NF * (n - 1) + 1 + START)
                        for m in range(2):
                            for j, t in enumerate(tiles):
                                for k in range(KD):
                                    at = (m * KD + k) * FF + t * P
                                    w = W.ffn[:, at:at + P]
                                    dst = FB[2 * (f % 2) + m][:, j * P:(j + 1) * P]
                                    nc.tensor.matmul(dst, w, x2h[:, k * P:(k + 1) * P], start=(k == 0), stop=False)
                                    ins = nc.tensor.matmul(dst, w, x2l[:, k * P:(k + 1) * P], start=False,
                                                           stop=(k == KD - 1))
                        ins.then_inc(f1, 1)
                if attn:
                    for c in range(1 + KV):
                        pe.wait_ge(q_ready, 5 * n + c + 1)
                        if c == 0:
                            pass
                        elif c == 1:
                            if ffn:
                                pe.wait_ge(x2_lo, n)
                        else:
                            pe.wait_ge(qkt_out, 5 * n + c - 1)
                        transpose(TR[c % 2], rope[:, c, :], qkt)
                    pe.wait_ge(qkt_out, 5 * n + 5)
                    if ffn:
                        pe.wait_ge(gated, NF * (n - 1) + 2 + START)
                    for h in range(KV):
                        for b in range(BT):
                            at = h * P + b * SEQ
                            ins = nc.tensor.matmul(SCORES[:, at:at + SEQ], qT[:, h, b * P:(b + 1) * P],
                                                   kT[:, h, b * SEQ:(b + 1) * SEQ], start=True, stop=True)
                    ins.then_inc(scored, 1)
                if ffn:
                    if attn:
                        pe.wait_ge(squared, 5 * n + 5)
                        pe.wait_ge(roped_b, 5 * n + 5)
                    else:
                        pe.wait_ge(o_out, n - 1 + START)
                    pe.wait_ge(hid_hi, NF * n)
                    pe.wait_ge(hid_lo, NF * n)
                    for k in range(KF):
                        at = 2 * KD * FF + k * D
                        nc.tensor.matmul(PROJ[0][:, :], hh[:, k, :], W.ffn[:, at:at + D], start=(k == 0), stop=False)
                        ins = nc.tensor.matmul(PROJ[0][:, :], hl[:, k, :], W.ffn[:, at:at + D], start=False,
                                               stop=(k == KF - 1))
                    ins.then_inc(w3, 1)
                if attn:
                    pe.wait_ge(soft, 4 * n + 4)
                    transpose(TR[1], pr[:, :, :].rearrange("p u k -> p (u k)"), pt)
                    pe.wait_ge(v_out, n + 1)
                    for h in range(KV):
                        pe.wait_ge(pbd_out, KV * n + h + 1)
                        if h == 0 and ffn:
                            pe.wait_ge(gated, NF * n + START)
                        if h == KV - 1:
                            pe.wait_ge(c_lo, KV * n + 1)
                        nc.tensor.matmul(PV_BANK[h][:, :], v[:, h * HD:(h + 1) * HD],
                                         pbd[:, h, :, :].rearrange("p b q -> p (b q)"), start=True, stop=True
                                         ).then_inc(pv, 1)
                    pairs = []
                    pe.wait_ge(c_hi, KV * (n + 1))
                    pe.wait_ge(c_lo, KV * (n + 1))
                    for k in range(HEADS):
                        at = O_AT + k * D
                        pairs.append((ch[:, k, :], cl[:, k, :], W.a_hi[:, at:at + D], W.a_lo[:, at:at + D]))
                    split_products(PROJ[1][:, :], pairs, o_sum)

            over_tiles(pe, body)


class Weights:

    def __init__(self, a_hi, a_lo, ffn, scale, eps_q, eps_k, o_unscale):
        self.a_hi, self.a_lo, self.ffn = a_hi, a_lo, ffn
        self.scale, self.eps_q, self.eps_k, self.o_unscale = scale, eps_q, eps_k, o_unscale


def program(nc, x, vt, w_attn, w_ffn, tables, norm_w, mask, own, ident, out):
    h1 = nc.dram_tensor("h1_rows", (TOK, D), FP32, kind="Internal").ap()
    token_attention(nc, x, vt, h1, ident)
    with ExitStack() as ctx:
        def sb(name, shape, dt=FP32):
            return ctx.enter_context(nc.sbuf_tensor(name, shape, dt))

        W = Weights(sb("attn_hi", [P, ATTN_W], F16), sb("attn_lo", [P, ATTN_W], F16), sb("ffn_w", [P, FFN_W], F16),
                    sb("w_scale", [P, 4]), sb("eps_q", [P, 1]), sb("eps_k", [P, 1]), sb("o_unscale", [P, 1]))
        weights(nc, W, w_attn, w_ffn)
        blocks(nc, W, h1, tables, norm_w, mask, own, ident, out)


_OUTS = [((B, CH, T), "float32")]


def _constants():
    inv_freq = (1.0 / np.float32(10000.0) ** (np.arange(0, HD, 2, dtype=np.float32) / HD)).astype(np.float32)
    freqs = np.arange(SEQ, dtype=np.float32)[:, None] * inv_freq[None, :]
    emb = np.concatenate([freqs, freqs], axis=-1)
    cos, sin = np.cos(emb).astype(np.float32), np.sin(emb).astype(np.float32)
    sin[:, :HD // 2] *= -1.0
    rotary = np.tile(np.stack([cos, sin, cos, sin], axis=1), (BT, 1, 1))
    t = np.arange(P)[:, None] % SEQ
    mask = np.where(np.arange(SEQ)[None, :] <= t, 0.0, -1e30).astype(np.float32)
    own = (np.arange(P)[:, None] // SEQ == np.arange(BT)[None, :]).astype(np.float32)
    return rotary.astype(np.float32), mask, own, np.eye(P, dtype=np.float32)


def _tiled(w):
    return w.reshape(-1, P, w.shape[1]).transpose(1, 0, 2).reshape(P, -1)


def kernel(**inputs):
    import concourse.bacc as _bacc
    from concourse.bass_utils import run_bass_kernel_spmd as _run

    a = {k: np.asarray(v) for k, v in inputs.items()}
    rotary, mask, own, ident = _constants()
    v = a["x"][:, 2 * CH:].reshape(NG, GB, CH, NT, P)
    qn, kn = a["L0_attn_qn_w"], a["L0_attn_kn_w"]
    halves = [np.concatenate([w[HD // 2:], w[:HD // 2]]) for w in (qn, kn)]
    arrays = {
        "x": a["x"],
        "v_t": v.transpose(0, 4, 3, 1, 2).reshape(NG, P, T),
        "w_attn": np.concatenate([_tiled(a[f"L0_attn_{n}"].T) for n in ("Wq", "Wk", "Wv", "Wo")], axis=1),
        "w_ffn": np.concatenate([_tiled(a[f"L0_ffn_{n}"].T) for n in ("w1", "w2", "w3")], axis=1),
        "rotary": rotary,
        "norm_weights": np.broadcast_to(np.stack([qn, halves[0], kn, halves[1]]), (P, 4, HD)),
        "causal": mask,
        "own": own,
        "identity": ident,
    }
    arrays = {k: np.ascontiguousarray(v) for k, v in arrays.items()}
    nc = _bacc.Bacc("TRN2", target_bir_lowering=False, num_devices=1)
    args = [nc.dram_tensor(f"in_{k}", v.shape, mybir.dt.from_np(v.dtype), kind="ExternalInput").ap()
            for k, v in arrays.items()]
    out = nc.dram_tensor("out", _OUTS[0][0], FP32, kind="ExternalOutput").ap()
    program(nc, *args, out.rearrange("b c t -> (b c) t"))
    r = _run(nc, [{f"in_{k}": v for k, v in arrays.items()}], core_ids=[0])
    return r.results[0]["out"]
```

```python
import numpy as np
import concourse.bass as bass
from concourse import mybir
from contextlib import ExitStack

FP32 = mybir.dt.float32
F32R = mybir.dt.float32r
F16 = mybir.dt.float16
I32 = mybir.dt.int32
ALU = mybir.AluOpType
ACT = mybir.ActivationFunctionType
AX = mybir.AxisListType
MAX_OP = bass.bass_isa.ReduceOp.max
ADD_OP = bass.bass_isa.ReduceOp.add

B, CH, T = 64, 32, 512
P = 128
GB = P // CH
NG = B // GB
NT = T // P
STEPS = GB * NT
DMA = 16
START = 1
TOK_SCALE = float(np.float32(1.0 / np.sqrt(np.sqrt(32.0)))) ** 2


def token_attention(nc, x, vt, h1, ident_in):
    with ExitStack() as ctx:
        def sb(name, shape, dt=FP32):
            return ctx.enter_context(nc.sbuf_tensor(name, shape, dt))

        def pb(name):
            return ctx.enter_context(nc.psum_tensor(name, [P, T], FP32))

        def sem(name):
            return ctx.enter_context(nc.semaphore(name))

        NB = 3
        QP = [sb(f"q_parts{n}", [P, GB, T], F32R) for n in range(NB)]
        KP = [sb(f"k_parts{n}", [P, GB, T], F32R) for n in range(NB)]
        VT = [sb(f"v_t{n}", [P, NT, P]) for n in range(NB)]
        q_raw = sb("q_raw", [P, GB, T])
        k_raw = sb("k_raw", [P, GB, T])
        NE = 3 * GB
        E = sb("exps", [P, NE, T])
        ident = sb("tok_ident", [P, P])
        ones = sb("tok_ones", [P, CH])
        row_max = sb("row_max", [P, STEPS])
        max_parts = sb("max_parts", [P, 2, STEPS], F32R)
        max_t = sb("max_t", [2 * STEPS, P])
        rden = sb("tok_rden", [P, T])
        h_tile = sb("h_tile", [P, T])
        den = sb("tok_den_sum", [P, T])
        out = sb("tok_out_sum", [P, T])

        S = [pb(f"score_rows{n}") for n in range(2)]
        ST = [pb(f"score_cols{n}") for n in range(3)]
        OUT = pb("tok_out")
        DEN = pb("tok_den")
        MT = pb("max_transposed")

        ident_in_sem = sem("t_ident_in")
        const_set = sem("t_const_set")
        q_in, k_in = sem("t_q_in"), sem("t_k_in")
        v_in = [sem(f"t_v_in{n}") for n in range(NB)]
        hi_done, q_lo, k_lo = sem("t_hi_done"), sem("t_q_lo"), sem("t_k_lo")
        s_done, max_done, max_split = sem("t_s_done"), sem("t_max_done"), sem("t_max_split")
        mt_done, mt_out, max_in = sem("t_mt_done"), sem("t_mt_out"), sem("t_max_in")
        st_done, exp_done, pv_done = sem("t_st_done"), sem("t_exp_done"), sem("t_pv_done")
        sums_out, rden_done, h_done, h_out = sem("t_sums_out"), sem("t_rden_done"), sem("t_h_done"), sem("t_h_out")
        EXP_CREDIT = 3
        PV_CREDIT = 3

        AHEAD = 6
        MAX_AT = 2 + STEPS - AHEAD
        FINISHED = 4
        VALUES_AT = [6, 8, 9, 11, 12, 14, 16, 17]
        SPLIT_AT = [2, 4, 6, 8]
        PEEL = NG - 4
        block = ctx.enter_context(nc.Block())

        def over_groups(eng, body):
            with eng.Fori(0, PEEL // NB) as j:
                for p in range(NB):
                    body(j * NB + p, p, True, True)
            for g in range(PEEL, NG):
                body(g, g % NB, g + 1 < NG, g + 2 < NG)

        @block.sync
        def _(sp):
            def load_qk(g):
                for raw, lo, done, first in ((q_raw, q_lo, q_in, 0), (k_raw, k_lo, k_in, CH)):
                    sp.wait_ge(lo, g)
                    for r in range(3):
                        sp.dma_start(raw[r * CH:(r + 1) * CH, :, :],
                                     x[bass.ds(g * GB, GB), first:first + CH, :].rearrange("b c t -> c b t")
                                     ).then_inc(done, DMA)

            def load_v(g, p):
                sp.dma_start(VT[p][:, :, :], vt[bass.ds(g, 1), :, :].rearrange("g s n -> (g s) n")
                             ).then_inc(v_in[p], DMA)

            def store_max(g, p):
                sp.wait_ge(mt_out, g + 1)
                for part in range(2):
                    row = QP[p][3 * CH + part:3 * CH + part + 1, :, :].bitcast(FP32)
                    sp.dma_start(row,
                                 max_t[part * STEPS:(part + 1) * STEPS, :]).then_inc(max_in, DMA)

            sp.dma_start(ident[:, :], ident_in).then_inc(ident_in_sem, DMA)
            load_qk(0)
            load_v(0, 0)
            load_qk(1)
            load_v(1, 1)
            load_qk(2)
            store_max(0, 0)

            def body(g, p, more, more2):
                if more2:
                    sp.wait_ge(pv_done, NT * g + PV_CREDIT)
                    load_v(g + 2, (p + 2) % NB)
                if more:
                    store_max(g + 1, (p + 1) % NB)
                if more2 and not (isinstance(g, int) and g + 3 >= NG):
                    load_qk(g + 3)
                sp.wait_ge(h_done, g + 1 + START)
                sp.dma_start(h1[bass.ds(g * P, P), :], h_tile[:, :]).then_inc(h_out, DMA)

            over_groups(sp, body)
            sp.wait_ge(h_out, NG * DMA + START)

        @block.gpsimd
        def _(pool):
            def split_lo(g, p):
                pool.wait_ge(hi_done, 4 * g + 2)
                nc.gpsimd.tensor_tensor(QP[p][CH:2 * CH, :, :], q_raw[CH:2 * CH, :, :],
                                        QP[p][CH:2 * CH, :, :].bitcast(FP32), ALU.subtract).then_inc(q_lo, 1)
                pool.wait_ge(hi_done, 4 * g + 4)
                nc.gpsimd.tensor_tensor(KP[p][2 * CH:3 * CH, :, :], k_raw[2 * CH:3 * CH, :, :],
                                        KP[p][2 * CH:3 * CH, :, :].bitcast(FP32), ALU.subtract).then_inc(k_lo, 1)

            split_lo(0, 0)
            split_lo(1, 1)

            def body(g, p, more, more2):
                if more2:
                    split_lo(g + 2, (p + 2) % NB)

            over_groups(pool, body)

        @block.scalar
        def _(act):
            def split_hi(g, p, n):
                raw, parts, done = ((q_raw, QP[p], q_in), (k_raw, KP[p], k_in))[n // 2]
                two = slice(2 * (n % 2), 2 * (n % 2) + 2)
                if n % 2 == 0:
                    act.wait_ge(done, 3 * DMA * (g + 1))
                nc.scalar.copy(parts[0:3 * CH, two, :], raw[0:3 * CH, two, :]).then_inc(hi_done, 1)

            for g in range(2):
                for n in range(4):
                    split_hi(g, g, n)

            def exps(g, p, u):
                act.wait_ge(st_done, STEPS * g + u + 1)
                if u % GB == 0:
                    act.wait_ge(pv_done, NT * g + u // GB - 2 + PV_CREDIT)
                nc.scalar.activation(E[:, (STEPS * p + u) % NE, :], ST[(p + u) % 3][:, :], ACT.Exp,
                                     scale=TOK_SCALE).then_inc(exp_done, 1)

            act.sem_inc(sums_out, START)
            act.wait_ge(pv_done, PV_CREDIT)
            exps(0, 0, 0)
            exps(0, 0, 1)

            def body(g, p, more, more2):
                for u in range(2, STEPS + 2):
                    if more2 and u in SPLIT_AT:
                        split_hi(g + 2, (p + 2) % NB, SPLIT_AT.index(u))
                    if u < STEPS:
                        exps(g, p, u)
                    elif more:
                        exps(g + 1, (p + 1) % NB, u - STEPS)
                act.wait_ge(pv_done, NT * (g + 1) + PV_CREDIT)
                act.wait_ge(h_done, g + START)
                nc.scalar.copy(den[:, :], DEN[:, :]).then_inc(sums_out, 1)
                nc.scalar.copy(out[:, :], OUT[:, :]).then_inc(sums_out, 1)

            over_groups(act, body)

        @block.vector
        def _(dve):
            def maximum(g, k):
                dve.wait_ge(s_done, STEPS * g + k + 1)
                nc.vector.reduce_max(row_max[:, k:k + 1], S[k % 2][:, :], AX.X).then_inc(max_done, 1)

            def split_maxima(g):
                dve.wait_ge(max_done, STEPS * (g + 1))
                nc.vector.tensor_scalar(max_parts[:, 0, :], row_max[:, :], -1.0, None, ALU.mult
                                        ).then_inc(max_split, 1)
                dve.wait_ge(max_split, 2 * g + 1)
                nc.vector.scalar_tensor_tensor(max_parts[:, 1, :], row_max[:, :], -1.0,
                                               max_parts[:, 0, :].bitcast(FP32), ALU.mult, ALU.subtract
                                               ).then_inc(max_split, 1)

            def take_transposed(g):
                dve.wait_ge(mt_done, g + 1)
                dve.wait_ge(max_in, 2 * DMA * g)
                nc.vector.tensor_copy(max_t[:, :], MT[0:2 * STEPS, 0:P]).then_inc(mt_out, 1)

            nc.vector.memset(ones[:, :], 1.0).then_inc(const_set, 1)
            for n in range(NB):
                nc.vector.memset(KP[n][3 * CH:3 * CH + 2, :, :].bitcast(FP32), 1.0).then_inc(const_set, 1)
            dve.sem_inc(h_done, START)
            dve.sem_inc(h_out, START)
            for k in range(STEPS):
                maximum(0, k)
            split_maxima(0)
            take_transposed(0)
            EARLY = AHEAD + 2 * FINISHED
            for k in range(EARLY):
                maximum(1, k)

            def body(g, p, more, more2):
                if more:
                    for k in range(EARLY, STEPS):
                        maximum(g + 1, k)
                    split_maxima(g + 1)
                    take_transposed(g + 1)
                    if more2:
                        for k in range(AHEAD):
                            maximum(g + 2, k)
                dve.wait_ge(sums_out, 2 * g + 1 + START)
                for n in range(FINISHED):
                    part = slice(n * T // FINISHED, (n + 1) * T // FINISHED)
                    nc.vector.reciprocal(rden[:, part], den[:, part]).then_inc(rden_done, 1)
                    if more2:
                        maximum(g + 2, AHEAD + 2 * n)
                        maximum(g + 2, AHEAD + 2 * n + 1)
                dve.wait_ge(rden_done, FINISHED * (g + 1))
                dve.wait_ge(sums_out, 2 * g + 2 + START)
                dve.wait_ge(h_out, DMA * g + START)
                nc.vector.tensor_tensor(h_tile[:, :], out[:, :], rden[:, :], ALU.mult).then_inc(h_done, 1)

            over_groups(dve, body)

        @block.tensor
        def _(pe):
            def rows(g, p, k):
                b, t = k // NT, k % NT
                if k == 0:
                    pe.wait_ge(q_lo, g + 1)
                    pe.wait_ge(k_lo, g + 1)
                if not (isinstance(g, int) and STEPS * g + k < 2):
                    pe.wait_ge(max_done, STEPS * g + k - 1)
                nc.tensor.matmul(S[k % 2][:, :], QP[p][0:3 * CH, b, t * P:(t + 1) * P], KP[p][0:3 * CH, b, :],
                                 start=True, stop=True).then_inc(s_done, 1)

            def transpose_maxima(g):
                pe.wait_ge(max_split, 2 * (g + 1))
                pe.wait_ge(mt_out, g)
                nc.tensor.matmul(MT[0:2 * STEPS, 0:P], max_parts[:, :, :].bitcast(FP32), ident[:, :],
                                 start=True, stop=True).then_inc(mt_done, 1)

            def cols(g, p, u):
                i, b = u // GB, u % GB
                if u == 0:
                    pe.wait_ge(max_in, 2 * DMA * (g + 1))
                pe.wait_ge(exp_done, STEPS * g + u - 2 + EXP_CREDIT)
                nc.tensor.matmul(ST[(p + u) % 3][:, :], KP[p][0:3 * CH + 2, b, i * P:(i + 1) * P],
                                 QP[p][0:3 * CH + 2, b, :], start=True, stop=True).then_inc(st_done, 1)

            def values(g, p, i, sums):
                if i == 0 and not sums:
                    pe.wait_ge(sums_out, 2 * g + START)
                    pe.wait_ge(v_in[p], g_over(g, p))
                pe.wait_ge(exp_done, STEPS * g + GB * (i + 1) + EXP_CREDIT)
                for b in range(GB):
                    into, by = (DEN, ones[:, :]) if sums else (OUT, VT[p][:, i, b * CH:(b + 1) * CH])
                    last = nc.tensor.matmul(into[b * CH:(b + 1) * CH, :], by, E[:, (STEPS * p + GB * i + b) % NE, :],
                                            start=(i == 0), stop=(i == NT - 1))
                if sums:
                    last.then_inc(pv_done, 1)

            turns = {}

            def g_over(g, p):
                if isinstance(g, int):
                    return DMA * (g // NB + 1)
                return DMA * (turns["j"] + 1)

            pe.wait_ge(ident_in_sem, DMA)
            pe.wait_ge(const_set, 1 + NB)
            for _ in range(EXP_CREDIT):
                pe.sem_inc(exp_done, 1)
            for _ in range(PV_CREDIT):
                pe.sem_inc(pv_done, 1)
            for k in range(STEPS):
                rows(0, 0, k)
            transpose_maxima(0)
            cols(0, 0, 0)
            cols(0, 0, 1)
            for k in range(AHEAD):
                rows(1, 1, k)

            def body(g, p, more, more2):
                q = (p + 1) % NB
                for u in range(2, STEPS + 2):
                    if more and u == MAX_AT:
                        transpose_maxima(g + 1)
                    if u < MAX_AT and more:
                        rows(g + 1, q, u - 2 + AHEAD)
                    if u >= MAX_AT and more2:
                        rows(g + 2, (p + 2) % NB, u - MAX_AT)
                    if u < STEPS:
                        cols(g, p, u)
                    elif more:
                        cols(g + 1, q, u - STEPS)
                    if u in VALUES_AT:
                        values(g, p, *divmod(VALUES_AT.index(u), 2))

            with pe.Fori(0, PEEL // NB) as j:
                turns["j"] = j
                for p in range(NB):
                    body(j * NB + p, p, True, True)
            for g in range(PEEL, NG):
                body(g, g % NB, g + 1 < NG, g + 2 < NG)


D = 512
KD = D // P
TOK = 64 * 32
NTT = TOK // P
SEQ = 32
BT = P // SEQ
HEADS, KV, HD = 16, 4, 128
G = HEADS // KV
FF = 1408
KF = FF // P
QKV_W = KD * (HEADS + 2 * KV) * HD
Q_AT, K_AT, V_AT, O_AT = 0, KD * HEADS * HD, KD * (HEADS + KV) * HD, QKV_W
ATTN_W = QKV_W + HEADS * D
FFN_W = 3 * KD * FF
X_SCALE = 2.0 ** 11
V_SHIFT = 2.0 ** -16
LN_EPS, RMS_EPS, GAMMA_EPS = 1e-5, 1e-6, 1e-8
A_CHUNK, F_CHUNK = 1024, FF
A_CHUNKS, F_CHUNKS = ATTN_W // A_CHUNK, FFN_W // F_CHUNK
ATTN_PARTS = ((Q_AT, K_AT), (K_AT, V_AT), (V_AT, O_AT), (O_AT, ATTN_W))


def weights(nc, W, w_attn, w_ffn):
    with ExitStack() as ctx:
        def sb(name, shape, dt=FP32):
            return ctx.enter_context(nc.sbuf_tensor(name, shape, dt))

        def sem(name):
            return ctx.enter_context(nc.semaphore(name))

        RING = 2
        raw_a = [sb(f"raw_attn{n}", [P, A_CHUNK]) for n in range(RING)]
        raw_f = [sb(f"raw_ffn{n}", [P, F_CHUNK]) for n in range(RING)]
        below = sb("w_below", [P, F_CHUNK], F16)
        amax = sb("w_amax", [P, A_CHUNKS])
        fsum = sb("w_fsum", [P, F_CHUNKS])
        amax4 = sb("w_amax4", [P, 4])
        fsum3 = sb("w_fsum3", [P, 3])
        amax_all = sb("w_amax_all", [P, 4])
        fsum_all = sb("w_fsum_all", [P, 3])
        thr = sb("w_thr", [P, 3])
        nthr = sb("w_nthr", [P, 3])
        tmp = sb("w_tmp", [P, 4])
        pow2 = sb("w_pow2", [P, 4])

        a_in = [sem(f"w_a_in{n}") for n in range(RING)]
        f_in = [sem(f"w_f_in{n}") for n in range(RING)]
        a_stat, f_stat = sem("w_a_stat"), sem("w_f_stat")
        folded, reduced, chain = sem("w_folded"), sem("w_reduced"), sem("w_chain")
        a_hi, a_lo, f_done = sem("w_a_hi"), sem("w_a_lo"), sem("w_f_done")
        block = ctx.enter_context(nc.Block())

        @block.sync
        def _(sp):
            for again, (a_free, f_free) in enumerate(((a_stat, f_stat), (a_lo, f_done))):
                with sp.Fori(0, A_CHUNKS // RING) as j:
                    for n in range(RING):
                        if again:
                            sp.wait_ge(a_stat, A_CHUNKS + START)
                        sp.wait_ge(a_free, j * RING + START)
                        sp.dma_start(raw_a[n][:, :], w_attn[:, bass.ds((j * RING + n) * A_CHUNK, A_CHUNK)]
                                     ).then_inc(a_in[n], DMA)
                with sp.Fori(0, F_CHUNKS // RING) as j:
                    for n in range(RING):
                        if again:
                            sp.wait_ge(f_stat, F_CHUNKS + START)
                        sp.wait_ge(f_free, j * RING + START)
                        sp.dma_start(raw_f[n][:, :], w_ffn[:, bass.ds((j * RING + n) * F_CHUNK, F_CHUNK)]
                                     ).then_inc(f_in[n], DMA)

        @block.gpsimd
        def _(pool):
            pool.wait_ge(folded, 7)
            nc.gpsimd.partition_all_reduce(amax_all[:, :], amax4[:, :], P, MAX_OP
                                           ).then_inc(reduced, 1)
            pool.wait_ge(reduced, 1)
            nc.gpsimd.partition_all_reduce(fsum_all[:, :], fsum3[:, :], P, ADD_OP).then_inc(reduced, 1)

        @block.vector
        def _(dve):
            for start in (a_stat, f_stat, a_lo, f_done):
                dve.sem_inc(start, START)
            with dve.Fori(0, A_CHUNKS // RING) as j:
                for n in range(RING):
                    dve.wait_ge(a_in[n], DMA * (j + 1))
                    nc.vector.tensor_reduce(amax[:, bass.ds(j * RING + n, 1)], raw_a[n][:, :], AX.X, ALU.max,
                                            apply_absolute_value=True).then_inc(a_stat, 1)
            with dve.Fori(0, F_CHUNKS // RING) as j:
                for n in range(RING):
                    dve.wait_ge(f_in[n], DMA * (j + 1))
                    nc.vector.tensor_reduce(fsum[:, bass.ds(j * RING + n, 1)], raw_f[n][:, :], AX.X, ALU.add,
                                            apply_absolute_value=True).then_inc(f_stat, 1)
            dve.wait_ge(a_stat, A_CHUNKS + START)
            dve.wait_ge(f_stat, F_CHUNKS + START)
            for m, (lo, hi) in enumerate(ATTN_PARTS):
                nc.vector.tensor_reduce(amax4[:, m:m + 1], amax[:, lo // A_CHUNK:hi // A_CHUNK], AX.X, ALU.max
                                        ).then_inc(folded, 1)
            for m in range(3):
                nc.vector.tensor_reduce(fsum3[:, m:m + 1], fsum[:, m * KD:(m + 1) * KD], AX.X, ALU.add
                                        ).then_inc(folded, 1)
            steps = [0]

            def link(ins):
                steps[0] += 1
                ins.then_inc(chain, 1)
                dve.wait_ge(chain, steps[0])

            dve.wait_ge(reduced, 2)
            link(nc.vector.tensor_scalar(tmp[:, :], amax_all[:, :], 1e-30, None, ALU.max))
            link(nc.vector.tensor_scalar(pow2[:, :].bitcast(I32), tmp[:, :].bitcast(I32), 0x7f800000, None,
                                         ALU.bitwise_and))
            link(nc.vector.reciprocal(tmp[:, :], pow2[:, :]))
            link(nc.vector.tensor_scalar(W.scale[:, :], tmp[:, :], 2.0 ** 10, None, ALU.mult))
            link(nc.vector.tensor_tensor(tmp[:, :], W.scale[:, :], W.scale[:, :], ALU.mult))
            link(nc.vector.tensor_scalar(W.eps_q[:, :], tmp[:, 0:1], HD * RMS_EPS * X_SCALE ** 2, None, ALU.mult))
            link(nc.vector.tensor_scalar(W.eps_k[:, :], tmp[:, 1:2], RMS_EPS * X_SCALE ** 2, None, ALU.mult))
            link(nc.vector.tensor_tensor(tmp[:, 0:1], pow2[:, 2:3], pow2[:, 3:4], ALU.mult))
            link(nc.vector.tensor_scalar(W.o_unscale[:, :], tmp[:, 0:1], 2.0 ** -15, None, ALU.mult))
            link(nc.vector.tensor_scalar(tmp[:, 0:3], fsum_all[:, :], 1.0 / (FF * D), GAMMA_EPS, ALU.mult, ALU.add))
            link(nc.vector.tensor_scalar(thr[:, :], tmp[:, 0:3], 0.5, None, ALU.mult))
            link(nc.vector.tensor_scalar(nthr[:, :], tmp[:, 0:3], -0.5, None, ALU.mult))
            for m, (lo, hi) in enumerate(ATTN_PARTS):
                with dve.Fori(lo // A_CHUNK // RING, hi // A_CHUNK // RING) as j:
                    for n in range(RING):
                        c = j * RING + n
                        dve.wait_ge(a_hi, c + 1)
                        nc.vector.scalar_tensor_tensor(W.a_lo[:, bass.ds(c * A_CHUNK, A_CHUNK)], raw_a[n][:, :],
                                                       W.scale[:, m:m + 1], W.a_hi[:, bass.ds(c * A_CHUNK, A_CHUNK)],
                                                       ALU.mult, ALU.subtract).then_inc(a_lo, 1)
            for m in range(3):
                with dve.Fori(m * KD // RING, (m + 1) * KD // RING) as j:
                    for n in range(RING):
                        c = j * RING + n
                        dve.wait_ge(f_in[n], DMA * (j + 1 + F_CHUNKS // RING))
                        nc.vector.tensor_scalar(below[:, :], raw_f[n][:, :], nthr[:, m:m + 1], None, ALU.is_lt
                                                ).then_inc(f_stat, 1)
                        dve.wait_ge(f_stat, F_CHUNKS + c + 1 + START)
                        nc.vector.scalar_tensor_tensor(W.ffn[:, bass.ds(c * F_CHUNK, F_CHUNK)], raw_f[n][:, :],
                                                       thr[:, m:m + 1], below[:, :], ALU.is_gt, ALU.subtract
                                                       ).then_inc(f_done, 1)
                        dve.wait_ge(f_done, c + 1 + START)

        @block.scalar
        def _(act):
            act.wait_ge(chain, 4)
            for m, (lo, hi) in enumerate(ATTN_PARTS):
                with act.Fori(lo // A_CHUNK // RING, hi // A_CHUNK // RING) as j:
                    for n in range(RING):
                        c = j * RING + n
                        act.wait_ge(a_in[n], DMA * (j + 1 + A_CHUNKS // RING))
                        nc.scalar.activation(W.a_hi[:, bass.ds(c * A_CHUNK, A_CHUNK)], raw_a[n][:, :], ACT.Copy,
                                             scale=W.scale[:, m:m + 1]).then_inc(a_hi, 1)


def blocks(nc, W, h1, tables_in, norm_in, mask_in, block_in, ident_in, out):
    with ExitStack() as ctx:
        def sb(name, shape, dt=FP32):
            return ctx.enter_context(nc.sbuf_tensor(name, shape, dt))

        def sem(name):
            return ctx.enter_context(nc.semaphore(name))

        PROJ = [ctx.enter_context(nc.psum_tensor(f"proj{n}", [P, D], FP32)) for n in range(2)]
        TR = [ctx.enter_context(nc.psum_tensor(f"transposed{n}", [P, D], FP32)) for n in range(2)]
        FB = [ctx.enter_context(nc.psum_tensor(f"ffn_sum{n}", [P, D], FP32)) for n in range(4)]
        PV_BANK = [FB[0], FB[1], FB[3], FB[0]]
        SCORES = FB[2]

        tables = sb("tables", [P, 4, HD])
        norm_w = sb("norm_w", [P, 4, HD])
        mask = sb("mask", [P, SEQ])
        own = sb("own_batch", [P, BT])
        ident = sb("ident", [P, P])
        minus_half = sb("minus_half", [P, HEADS])
        h_ln = sb("h_ln", [P, D])
        h_res = sb("h_res", [P, D])
        stats = sb("stats", [P, 2, 6])
        mv = sb("mv", [P, 2, 2])
        var = sb("var", [P, 2, 1])
        rstd = sb("rstd", [P, 2, 1])
        xn = sb("xn", [P, D])
        xh, xl = sb("x_hi", [P, D], F16), sb("x_lo", [P, D], F16)
        sq = [sb(f"squares{n}", [P, D]) for n in range(2)]
        ss = sb("sums_sq", [P, KV + HEADS])
        ms = sb("mean_sq", [P, KV + HEADS])
        rr = sb("rms_inv", [P, KV + HEADS])
        ra = [sb(f"rope_cos{n}", [P, D]) for n in range(2)]
        rb = [sb(f"rope_sin{n}", [P, D]) for n in range(2)]
        rope = sb("roped", [P, 1 + KV, D])
        kT = sb("k_t", [P, KV, P])
        qT = sb("q_t", [P, KV, G * P])
        v = sb("v", [P, KV * HD])
        sm = sb("scores", [P, HEADS, SEQ])
        sd = sb("scores_less_max", [P, HEADS, SEQ])
        pr = sb("probs", [P, HEADS, SEQ])
        mx = sb("row_maxima", [P, HEADS])
        den = sb("row_sums", [P, HEADS])
        rden = sb("row_sums_inv", [P, HEADS])
        pbd = sb("probs_blocks", [P, KV, BT, G * SEQ])
        ch, cl = sb("ctx_hi", [P, HEADS, P], F16), sb("ctx_lo", [P, HEADS, P], F16)
        h2 = sb("h2", [P, D])
        x2n = sb("x2n", [P, D])
        x2h, x2l = sb("x2_hi", [P, D], F16), sb("x2_lo", [P, D], F16)
        th = sb("tanh", [P, D])
        hid = sb("hidden", [P, D])
        hh, hl = sb("hidden_hi", [P, KF, P], F16), sb("hidden_lo", [P, KF, P], F16)
        o_tile = sb("out_tile", [P, D])

        const_in, const_set = sem("b_const_in"), sem("b_const_set")
        ln_in, res_in, out_done = sem("b_ln_in"), sem("b_res_in"), sem("b_out_done")
        ln1_var, ln1_rstd, ln1 = sem("b_ln1_var"), sem("b_ln1_rstd"), sem("b_ln1")
        ln2_var, ln2_rstd, ln2 = sem("b_ln2_var"), sem("b_ln2_rstd"), sem("b_ln2")
        xt, x_hi, x_lo = sem("b_xt"), sem("b_x_hi"), sem("b_x_lo")
        proj, squared, ssum, roped_a, roped_b = (sem("b_proj"), sem("b_squared"), sem("b_ssum"), sem("b_roped_a"),
                                                 sem("b_roped_b"))
        added, mean_sq, rms, q_ready, v_out = (sem("b_added"), sem("b_mean_sq"), sem("b_rms"), sem("b_q_ready"),
                                               sem("b_v_out"))
        qkt, qkt_out = sem("b_qkt"), sem("b_qkt_out")
        scored, masked, sub, exped, probs = (sem("b_scored"), sem("b_masked"), sem("b_sub"), sem("b_exped"),
                                             sem("b_probs"))
        soft = sem("b_soft")
        ln1_self, ln2_self = sem("b_ln1_self"), sem("b_ln2_self")
        pt, pbd_out, pv, c_hi, c_lo = sem("b_pt"), sem("b_pbd_out"), sem("b_pv"), sem("b_c_hi"), sem("b_c_lo")
        o_sum, h2_done = sem("b_o_sum"), sem("b_h2_done")
        xt2, x2_hi, x2_lo = sem("b_xt2"), sem("b_x2_hi"), sem("b_x2_lo")
        f1, tanhed, gated, hid_hi, hid_lo = (sem("b_f1"), sem("b_tanhed"), sem("b_gated"), sem("b_hid_hi"),
                                             sem("b_hid_lo"))
        w3, o_out = sem("b_w3"), sem("b_o_out")

        NPROJ = 2 + KV
        FG = [range(0, 4), range(4, 8), range(8, KF)]
        NF = len(FG)
        TRANSPOSE_AT = {(0, 0): [0], (0, 1): [1], (1, 0): [2, 3], (1, 1): [4]}
        SCORES_AT = (2, 0)
        DOWN_FIRST = 8
        block = ctx.enter_context(nc.Block())

        def over_tiles(eng, body):
            body(0, True, False)
            with eng.Fori(1, NTT - 1) as n:
                body(n, True, True)
            body(NTT - 1, True, True)
            body(NTT, False, True)

        def bcast(ap, shape, at):
            return ap.unsqueeze(at).to_broadcast(shape)

        @block.sync
        def _(sp):
            for dst, src in ((tables[:, :, :], tables_in), (norm_w[:, :, :], norm_in), (mask[:, :], mask_in),
                             (own[:, :], block_in), (ident[:, :], ident_in)):
                sp.dma_start(dst, src).then_inc(const_in, DMA)
            sp.dma_start(h_ln[:, :], h1[0:P, :]).then_inc(ln_in, DMA)

            def body(n, attn, ffn):
                if attn and not (isinstance(n, int) and n + 1 >= NTT):
                    sp.wait_ge(ln1, n + 1)
                    sp.dma_start(h_ln[:, :], h1[bass.ds((n + 1) * P, P), :]).then_inc(ln_in, DMA)
                if attn:
                    sp.wait_ge(h2_done, n)
                    sp.dma_start(h_res[:, :], h1[bass.ds(n * P, P), :]).then_inc(res_in, DMA)
                if ffn:
                    sp.wait_ge(o_out, n + START)
                    sp.dma_start(out[bass.ds((n - 1) * P, P), :], o_tile[:, :]).then_inc(out_done, DMA)

            over_tiles(sp, body)
            sp.wait_ge(out_done, DMA * NTT + START)

        @block.gpsimd
        def _(pool):
            def inv_std(n, m, var_done, out_sem):
                pool.wait_ge(var_done, n + 1)
                nc.gpsimd.tensor_tensor(rstd[:, m, :], var[:, m, :], minus_half[:, 0:1], ALU.pow).then_inc(out_sem, 1)

            pool.wait_ge(const_set, 2)
            inv_std(0, 0, ln1_var, ln1_rstd)

            def body(n, attn, ffn):
                if not attn:
                    return

                def add_parts(c):
                    pool.wait_ge(roped_b, 5 * n + c + 1)
                    nc.gpsimd.tensor_tensor(rope[:, c, :], ra[c % 2][:, :], rb[c % 2][:, :], ALU.add
                                            ).then_inc(added, 1)

                def invert(lo, hi, k):
                    pool.wait_ge(mean_sq, 2 * n + k + 1)
                    nc.gpsimd.tensor_tensor(rr[:, lo:hi], ms[:, lo:hi], minus_half[:, 0:hi - lo], ALU.pow
                                            ).then_inc(rms, 1)

                def normalise(c):
                    pool.wait_ge(added, 5 * n + c + 1)
                    view = rope[:, c, :].rearrange("p (h d) -> p h d", d=HD)
                    nc.gpsimd.tensor_tensor(view, view, bcast(rr[:, G * c:G * c + G], [P, G, HD], 2), ALU.mult
                                            ).then_inc(q_ready, 1)

                add_parts(0)
                invert(0, KV, 0)
                pool.wait_ge(rms, 2 * n + 1)
                normalise(0)
                for c in range(1, 1 + KV):
                    add_parts(c)
                invert(KV, KV + HEADS, 1)
                pool.wait_ge(rms, 2 * n + 2)
                for c in range(1, 1 + KV):
                    normalise(c)
                inv_std(n + 1, 0, ln1_var, ln1_rstd) if not (isinstance(n, int) and n + 1 >= NTT) else None
                inv_std(n, 1, ln2_var, ln2_rstd)

            over_tiles(pool, body)

        @block.scalar
        def _(act):
            def take_x(n):
                act.wait_ge(xt, n + 1)
                nc.scalar.copy(xh[:, :], TR[0][:, :]).then_inc(x_hi, 1)

            def square(n, c):
                act.wait_ge(proj, NPROJ * n + c + 1)
                if not (isinstance(n, int) and 5 * n + c < 2):
                    act.wait_ge(ssum, 5 * n + c - 1)
                nc.scalar.activation(sq[c % 2][:, :], PROJ[c % 2][:, :], ACT.Square).then_inc(squared, 1)

            def tanh(n, f):
                w = len(FG[f]) * P
                act.wait_ge(f1, 2 * NF * n + 2 * f + 1)
                act.wait_ge(gated, NF * n + f + START)
                nc.scalar.activation(th[:, 0:w], FB[2 * (f % 2)][:, 0:w], ACT.Tanh, scale=0.5 / X_SCALE
                                     ).then_inc(tanhed, 1)

            def hidden_hi(n, f):
                tiles = FG[f]
                act.wait_ge(gated, NF * n + f + 1 + START)
                nc.scalar.mul(hh[:, tiles[0]:tiles[-1] + 1, :].rearrange("p k t -> p (k t)"),
                              hid[:, 0:len(tiles) * P], 2.0 ** -6).then_inc(hid_hi, 1)

            def take_qk(n, c):
                act.wait_ge(qkt, 5 * n + c + 1)
                src = TR[c % 2][:, :]
                if c == 0:
                    nc.scalar.copy(kT[:, :, :].rearrange("p h t -> p (h t)"), src).then_inc(qkt_out, 1)
                else:
                    nc.scalar.copy(qT[:, c - 1, :].rearrange("p (b g t) -> p g b t", g=G, b=BT),
                                   src.rearrange("p (g b t) -> p g b t", g=G, b=BT)).then_inc(qkt_out, 1)

            take_x(0)

            def body(n, attn, ffn):
                last = isinstance(n, int) and n + 1 >= NTT
                if attn:
                    for c in range(KV):
                        square(n, c)
                if ffn:
                    act.wait_ge(xt2, n)
                    nc.scalar.copy(x2h[:, :], TR[1][:, :]).then_inc(x2_hi, 1)
                if attn:
                    square(n, KV)
                    act.wait_ge(proj, NPROJ * (n + 1))
                    nc.scalar.mul(v[:, :], PROJ[1][:, :], V_SHIFT).then_inc(v_out, 1)
                for f in range(NF):
                    for m in range(2):
                        if ffn and m == 0:
                            tanh(n - 1, f)
                        if attn:
                            for c in TRANSPOSE_AT.get((f, m), []):
                                take_qk(n, c)
                        if ffn and m == 1:
                            hidden_hi(n - 1, f)
                if attn:
                    act.wait_ge(sub, n + 1)
                    nc.scalar.activation(pr[:, :, :], sd[:, :, :], ACT.Exp).then_inc(exped, 1)
                    if not last:
                        take_x(n + 1)
                    for h in range(KV):
                        act.wait_ge(pv, KV * n + h + 1)
                        nc.scalar.copy(ch[:, G * h:G * h + G, :].rearrange("p g (b t) -> p b g t", b=BT),
                                       PV_BANK[h][:, :].rearrange("p (b g t) -> p b g t", g=G, b=BT)).then_inc(c_hi, 1)

            over_tiles(act, body)

        @block.vector
        def _(dve):
            for start in (o_out, gated, out_done):
                dve.sem_inc(start, START)
            nc.vector.memset(minus_half[:, :], -0.5).then_inc(const_set, 1)
            dve.wait_ge(const_in, 5 * DMA)
            nc.vector.scalar_tensor_tensor(tables[:, :, :], norm_w[:, :, :], 1.0, tables[:, :, :], ALU.add, ALU.mult
                                           ).then_inc(const_set, 1)

            def ln_stats(n, m, src, var_done, self_sem):
                nc.vector.bn_stats(stats[:, m, :], src).then_inc(self_sem, 1)
                dve.wait_ge(self_sem, 3 * n + 1)
                dve.sem_inc(self_sem, 1)
                nc.vector.bn_aggr(mv[:, m, :], stats[:, m, :]).then_inc(self_sem, 1)
                dve.wait_ge(self_sem, 3 * n + 3)
                nc.vector.tensor_scalar(var[:, m, :], mv[:, m, 1:2], LN_EPS, X_SCALE ** -2, ALU.add, ALU.mult
                                        ).then_inc(var_done, 1)

            def ln_apply(n, m, src, dst, rstd_done, done):
                dve.wait_ge(rstd_done, n + 1)
                nc.vector.tensor_scalar(dst, src, mv[:, m, 0:1], rstd[:, m, :], ALU.subtract, ALU.mult
                                        ).then_inc(done, 1)

            def x_low(n):
                dve.wait_ge(x_hi, n + 1)
                nc.vector.tensor_tensor(xl[:, :], TR[0][:, :], xh[:, :], ALU.subtract).then_inc(x_lo, 1)

            def rotate(n, c):
                dve.wait_ge(squared, 5 * n + c + 1)
                if not (isinstance(n, int) and 5 * n + c < 2):
                    dve.wait_ge(added, 5 * n + c - 1)
                w = 2 if c == 0 else 0
                y = PROJ[c % 2][:, :].rearrange("p (h d) -> p h d", d=HD)
                a = ra[c % 2][:, :].rearrange("p (h d) -> p h d", d=HD)
                b = rb[c % 2][:, :].rearrange("p (h d) -> p h d", d=HD)
                half = HD // 2
                nc.vector.tensor_tensor(a, y, bcast(tables[:, w, :], [P, G, HD], 1), ALU.mult).then_inc(roped_a, 1)
                nc.vector.tensor_tensor(b[:, :, 0:half], y[:, :, half:HD],
                                        bcast(tables[:, w + 1, 0:half], [P, G, half], 1), ALU.mult
                                        ).then_inc(roped_a, 1)
                nc.vector.tensor_tensor(b[:, :, half:HD], y[:, :, 0:half],
                                        bcast(tables[:, w + 1, half:HD], [P, G, half], 1), ALU.mult
                                        ).then_inc(roped_b, 1)
                nc.vector.tensor_reduce(ss[:, G * c:G * c + G], sq[c % 2][:, :].rearrange("p (h d) -> p h d", d=HD),
                                        AX.X, ALU.add).then_inc(ssum, 1)
                if c == 0:
                    dve.wait_ge(ssum, 5 * n + 1)
                    nc.vector.tensor_scalar(ms[:, 0:KV], ss[:, 0:KV], 1.0 / HD, W.eps_k[:, :], ALU.mult, ALU.add
                                            ).then_inc(mean_sq, 1)
                if c == KV:
                    dve.wait_ge(ssum, 5 * n + 5)
                    nc.vector.tensor_scalar(ms[:, KV:], ss[:, KV:], W.eps_q[:, :], None, ALU.add).then_inc(mean_sq, 1)

            def gate(n, f):
                w = len(FG[f]) * P
                dve.wait_ge(tanhed, NF * n + f + 1)
                dve.wait_ge(f1, 2 * NF * n + 2 * f + 2)
                nc.vector.scalar_tensor_tensor(hid[:, 0:w], th[:, 0:w], 1.0, FB[2 * (f % 2) + 1][:, 0:w],
                                               ALU.add, ALU.mult).then_inc(gated, 1)

            def hidden_lo(n, f):
                tiles = FG[f]
                dve.wait_ge(hid_hi, NF * n + f + 1)
                nc.vector.scalar_tensor_tensor(
                    hl[:, tiles[0]:tiles[-1] + 1, :].rearrange("p k t -> p (k t)"), hid[:, 0:len(tiles) * P], 2.0 ** -6,
                    hh[:, tiles[0]:tiles[-1] + 1, :].rearrange("p k t -> p (k t)"), ALU.mult, ALU.subtract
                ).then_inc(hid_lo, 1)
                dve.wait_ge(hid_lo, NF * n + f + 1)

            dve.wait_ge(const_set, 2)
            dve.wait_ge(ln_in, DMA)
            ln_stats(0, 0, h_ln[:, :], ln1_var, ln1_self)
            ln_apply(0, 0, h_ln[:, :], xn[:, :], ln1_rstd, ln1)
            x_low(0)

            def body(n, attn, ffn):
                last = isinstance(n, int) and n + 1 >= NTT
                if attn:
                    rotate(n, 0)
                if ffn:
                    ln_apply(n - 1, 1, h2[:, :], x2n[:, :], ln2_rstd, ln2)
                if attn:
                    for c in range(1, KV):
                        rotate(n, c)
                if ffn:
                    dve.wait_ge(x2_hi, n)
                    nc.vector.tensor_tensor(x2l[:, :], TR[1][:, :], x2h[:, :], ALU.subtract).then_inc(x2_lo, 1)
                if attn:
                    rotate(n, KV)
                    if not last:
                        dve.wait_ge(ln_in, DMA * (n + 2))
                        ln_stats(n + 1, 0, h_ln[:, :], ln1_var, ln1_self)
                if ffn:
                    for f in range(2):
                        gate(n - 1, f)
                        hidden_lo(n - 1, f)
                if attn:
                    if not last:
                        ln_apply(n + 1, 0, h_ln[:, :], xn[:, :], ln1_rstd, ln1)
                    step = [0]

                    def link(ins):
                        step[0] += 1
                        ins.then_inc(soft, 1)
                        dve.wait_ge(soft, 4 * n + step[0])

                    dve.wait_ge(scored, n + 1)
                    nc.vector.tensor_tensor(sm[:, :, :], SCORES[:, :].rearrange("p (u k) -> p u k", k=SEQ),
                                            bcast(mask[:, :], [P, HEADS, SEQ], 1), ALU.add).then_inc(masked, 1)
                    dve.wait_ge(masked, n + 1)
                    link(nc.vector.tensor_reduce(mx[:, :], sm[:, :, :], AX.X, ALU.max))
                    nc.vector.tensor_tensor(sd[:, :, :], sm[:, :, :], bcast(mx[:, :], [P, HEADS, SEQ], 2),
                                            ALU.subtract).then_inc(sub, 1)
                if ffn:
                    gate(n - 1, 2)
                if attn:
                    dve.wait_ge(exped, n + 1)
                    link(nc.vector.tensor_reduce(den[:, :], pr[:, :, :], AX.X, ALU.add))
                    link(nc.vector.reciprocal(rden[:, :], den[:, :]))
                    link(nc.vector.tensor_tensor(pr[:, :, :], pr[:, :, :], bcast(rden[:, :], [P, HEADS, SEQ], 2),
                                                 ALU.mult))
                if ffn:
                    hidden_lo(n - 1, 2)
                if attn:
                    dve.wait_ge(pt, n + 1)
                    for h in range(KV):
                        nc.vector.tensor_tensor(pbd[:, h, :, :],
                                                bcast(TR[1][:, h * P:(h + 1) * P], [P, BT, G * SEQ], 1),
                                                bcast(own[:, :], [P, BT, G * SEQ], 2), ALU.mult).then_inc(pbd_out, 1)
                        if h == 1 and not last:
                            x_low(n + 1)
                if ffn:
                    dve.wait_ge(w3, n)
                    dve.wait_ge(out_done, DMA * (n - 1) + START)
                    nc.vector.scalar_tensor_tensor(o_tile[:, :], PROJ[0][:, :], 2.0 ** -6, h2[:, :], ALU.mult, ALU.add
                                                   ).then_inc(o_out, 1)
                if attn:
                    for h in range(KV):
                        dve.wait_ge(c_hi, KV * n + h + 1)
                        nc.vector.tensor_tensor(cl[:, G * h:G * h + G, :].rearrange("p g (b t) -> p b g t", b=BT),
                                                PV_BANK[h][:, :].rearrange("p (b g t) -> p b g t", g=G, b=BT),
                                                ch[:, G * h:G * h + G, :].rearrange("p g (b t) -> p b g t", b=BT),
                                                ALU.subtract).then_inc(c_lo, 1)
                    dve.wait_ge(o_sum, n + 1)
                    dve.wait_ge(res_in, DMA * (n + 1))
                    nc.vector.scalar_tensor_tensor(h2[:, :], PROJ[1][:, :], W.o_unscale[:, :], h_res[:, :], ALU.mult,
                                                   ALU.add).then_inc(h2_done, 1)
                    dve.wait_ge(h2_done, n + 1)
                    ln_stats(n, 1, h2[:, :], ln2_var, ln2_self)

            over_tiles(dve, body)

        @block.tensor
        def _(pe):
            pe.wait_ge(const_in, 5 * DMA)

            def transpose(dst, src, last_sem):
                for k in range(KD):
                    t = nc.tensor.transpose(dst[:, k * P:(k + 1) * P], src[:, k * P:(k + 1) * P], ident[:, :])
                t.then_inc(last_sem, 1)

            def split_products(dst, pairs, done):
                for i, (ah, al, bh, bl) in enumerate(pairs):
                    nc.tensor.matmul(dst, ah, bh, start=(i == 0), stop=False)
                    nc.tensor.matmul(dst, ah, bl, start=False, stop=False)
                    t = nc.tensor.matmul(dst, al, bh, start=False, stop=(i == len(pairs) - 1))
                t.then_inc(done, 1)

            def project(n, c, first):
                if c == 0 and not first:
                    pe.wait_ge(o_out, n - 1 + START)
                if c == 1:
                    pe.wait_ge(h2_done, n)
                if c >= 2:
                    pe.wait_ge(squared, 5 * n + c - 1)
                    pe.wait_ge(roped_b, 5 * n + c - 1)
                pairs = []
                for k in range(KD):
                    at = (K_AT + k * KV * HD if c == 0 else V_AT + k * KV * HD if c == NPROJ - 1
                          else Q_AT + k * HEADS * HD + (c - 1) * D)
                    pairs.append((xh[:, k * P:(k + 1) * P], xl[:, k * P:(k + 1) * P],
                                  W.a_hi[:, at:at + D], W.a_lo[:, at:at + D]))
                split_products(PROJ[c % 2][:, :], pairs, proj)

            def transpose_x(n):
                pe.wait_ge(ln1, n + 1)
                pe.wait_ge(qkt_out, 5 * n)
                transpose(TR[0], xn, xt)

            def transpose_x2(n):
                pe.wait_ge(ln2, n + 1)
                pe.wait_ge(pbd_out, KV * (n + 1))
                transpose(TR[1], x2n, xt2)

            def gate_products(n, f, m):
                if f == 0 and m == 0:
                    pe.wait_ge(x2_hi, n + 1)
                    pe.wait_ge(x2_lo, n + 1)
                    pe.wait_ge(c_hi, KV * (n + 1))
                    pe.wait_ge(c_lo, KV * (n + 1))
                    pe.wait_ge(masked, n + 1)
                if f == 2:
                    pe.wait_ge(gated, NF * n + 1 + START)
                for j, t in enumerate(FG[f]):
                    for k in range(KD):
                        at = (m * KD + k) * FF + t * P
                        w = W.ffn[:, at:at + P]
                        dst = FB[2 * (f % 2) + m][:, j * P:(j + 1) * P]
                        nc.tensor.matmul(dst, w, x2h[:, k * P:(k + 1) * P], start=(k == 0), stop=False)
                        ins = nc.tensor.matmul(dst, w, x2l[:, k * P:(k + 1) * P], start=False, stop=(k == KD - 1))
                ins.then_inc(f1, 1)

            def transpose_qk(n, c, ffn):
                pe.wait_ge(q_ready, 5 * n + c + 1)
                if c == 1 and ffn:
                    pe.wait_ge(x2_lo, n)
                if c >= 2:
                    pe.wait_ge(qkt_out, 5 * n + c - 1)
                transpose(TR[c % 2], rope[:, c, :], qkt)

            def scores(n, ffn):
                pe.wait_ge(qkt_out, 5 * n + 5)
                if ffn:
                    pe.wait_ge(gated, NF * (n - 1) + 2 + START)
                for h in range(KV):
                    for b in range(BT):
                        at = h * P + b * SEQ
                        ins = nc.tensor.matmul(SCORES[:, at:at + SEQ], qT[:, h, b * P:(b + 1) * P],
                                               kT[:, h, b * SEQ:(b + 1) * SEQ], start=True, stop=True)
                ins.then_inc(scored, 1)

            def down_products(n, tiles):
                if tiles[0] == 0:
                    pe.wait_ge(squared, 5 * (n + 1) + 5) if not (isinstance(n, int) and n + 1 >= NTT) else None
                    pe.wait_ge(roped_b, 5 * (n + 1) + 5) if not (isinstance(n, int) and n + 1 >= NTT) else None
                    if isinstance(n, int) and n + 1 >= NTT:
                        pe.wait_ge(o_out, n + START)
                for k in tiles:
                    if k == 0 or k in (FG[1][0], FG[2][0]):
                        f = [g[0] for g in FG].index(k)
                        pe.wait_ge(hid_hi, NF * n + f + 1)
                        pe.wait_ge(hid_lo, NF * n + f + 1)
                    at = 2 * KD * FF + k * D
                    nc.tensor.matmul(PROJ[0][:, :], hh[:, k, :], W.ffn[:, at:at + D], start=(k == 0), stop=False)
                    ins = nc.tensor.matmul(PROJ[0][:, :], hl[:, k, :], W.ffn[:, at:at + D], start=False,
                                           stop=(k == KF - 1))
                if tiles[-1] == KF - 1:
                    ins.then_inc(w3, 1)

            def weigh_values(n, ffn):
                pe.wait_ge(v_out, n + 1)
                for h in range(KV):
                    pe.wait_ge(pbd_out, KV * n + h + 1)
                    if h == 0 and ffn:
                        pe.wait_ge(gated, NF * n + START)
                    if h == KV - 1:
                        pe.wait_ge(c_lo, KV * n + 1)
                    nc.tensor.matmul(PV_BANK[h][:, :], v[:, h * HD:(h + 1) * HD],
                                     pbd[:, h, :, :].rearrange("p b q -> p (b q)"), start=True, stop=True
                                     ).then_inc(pv, 1)

            def output_products(n):
                for k in range(HEADS):
                    if k % G == 0:
                        pe.wait_ge(c_hi, KV * n + k // G + 1)
                        pe.wait_ge(c_lo, KV * n + k // G + 1)
                    at = O_AT + k * D
                    ah, al = ch[:, k, :], cl[:, k, :]
                    bh, bl = W.a_hi[:, at:at + D], W.a_lo[:, at:at + D]
                    nc.tensor.matmul(PROJ[1][:, :], ah, bh, start=(k == 0), stop=False)
                    nc.tensor.matmul(PROJ[1][:, :], ah, bl, start=False, stop=False)
                    ins = nc.tensor.matmul(PROJ[1][:, :], al, bh, start=False, stop=(k == HEADS - 1))
                ins.then_inc(o_sum, 1)

            transpose_x(0)

            def body(n, attn, ffn):
                last = isinstance(n, int) and n + 1 >= NTT
                if attn:
                    pe.wait_ge(x_hi, n + 1)
                    pe.wait_ge(x_lo, n + 1)
                    for c in range(NPROJ - 2):
                        project(n, c, isinstance(n, int) and n == 0)
                if ffn:
                    transpose_x2(n - 1)
                if attn:
                    for c in range(NPROJ - 2, NPROJ):
                        project(n, c, False)
                for f in range(NF):
                    for m in range(2):
                        if ffn:
                            gate_products(n - 1, f, m)
                        if attn:
                            for c in TRANSPOSE_AT.get((f, m), []):
                                transpose_qk(n, c, ffn)
                            if (f, m) == SCORES_AT:
                                scores(n, ffn)
                if ffn:
                    down_products(n - 1, range(0, DOWN_FIRST))
                if attn:
                    pe.wait_ge(soft, 4 * n + 4)
                    transpose(TR[1], pr[:, :, :].rearrange("p u k -> p (u k)"), pt)
                if ffn:
                    down_products(n - 1, range(DOWN_FIRST, KF))
                if attn:
                    if not last:
                        transpose_x(n + 1)
                    weigh_values(n, ffn)
                    output_products(n)

            over_tiles(pe, body)


class Weights:

    def __init__(self, a_hi, a_lo, ffn, scale, eps_q, eps_k, o_unscale):
        self.a_hi, self.a_lo, self.ffn = a_hi, a_lo, ffn
        self.scale, self.eps_q, self.eps_k, self.o_unscale = scale, eps_q, eps_k, o_unscale


def program(nc, x, vt, w_attn, w_ffn, tables, norm_w, mask, own, ident, out):
    h1 = nc.dram_tensor("h1_rows", (TOK, D), FP32, kind="Internal").ap()
    token_attention(nc, x, vt, h1, ident)
    with ExitStack() as ctx:
        def sb(name, shape, dt=FP32):
            return ctx.enter_context(nc.sbuf_tensor(name, shape, dt))

        W = Weights(sb("attn_hi", [P, ATTN_W], F16), sb("attn_lo", [P, ATTN_W], F16), sb("ffn_w", [P, FFN_W], F16),
                    sb("w_scale", [P, 4]), sb("eps_q", [P, 1]), sb("eps_k", [P, 1]), sb("o_unscale", [P, 1]))
        weights(nc, W, w_attn, w_ffn)
        blocks(nc, W, h1, tables, norm_w, mask, own, ident, out)


_OUTS = [((B, CH, T), "float32")]


def _constants():
    inv_freq = (1.0 / np.float32(10000.0) ** (np.arange(0, HD, 2, dtype=np.float32) / HD)).astype(np.float32)
    freqs = np.arange(SEQ, dtype=np.float32)[:, None] * inv_freq[None, :]
    emb = np.concatenate([freqs, freqs], axis=-1)
    cos, sin = np.cos(emb).astype(np.float32), np.sin(emb).astype(np.float32)
    sin[:, :HD // 2] *= -1.0
    rotary = np.tile(np.stack([cos, sin, cos, sin], axis=1), (BT, 1, 1))
    t = np.arange(P)[:, None] % SEQ
    mask = np.where(np.arange(SEQ)[None, :] <= t, 0.0, -1e30).astype(np.float32)
    own = (np.arange(P)[:, None] // SEQ == np.arange(BT)[None, :]).astype(np.float32)
    return rotary.astype(np.float32), mask, own, np.eye(P, dtype=np.float32)


def _tiled(w):
    return w.reshape(-1, P, w.shape[1]).transpose(1, 0, 2).reshape(P, -1)


def kernel(**inputs):
    import concourse.bacc as _bacc
    from concourse.bass_utils import run_bass_kernel_spmd as _run

    a = {k: np.asarray(v) for k, v in inputs.items()}
    rotary, mask, own, ident = _constants()
    v = a["x"][:, 2 * CH:].reshape(NG, GB, CH, NT, P)
    qn, kn = a["L0_attn_qn_w"], a["L0_attn_kn_w"]
    halves = [np.concatenate([w[HD // 2:], w[:HD // 2]]) for w in (qn, kn)]
    arrays = {
        "x": a["x"],
        "v_t": v.transpose(0, 4, 3, 1, 2).reshape(NG, P, T),
        "w_attn": np.concatenate([_tiled(a[f"L0_attn_{n}"].T) for n in ("Wq", "Wk", "Wv", "Wo")], axis=1),
        "w_ffn": np.concatenate([_tiled(a[f"L0_ffn_{n}"].T) for n in ("w1", "w2", "w3")], axis=1),
        "rotary": rotary,
        "norm_weights": np.broadcast_to(np.stack([qn, halves[0], kn, halves[1]]), (P, 4, HD)),
        "causal": mask,
        "own": own,
        "identity": ident,
    }
    arrays = {k: np.ascontiguousarray(v) for k, v in arrays.items()}
    nc = _bacc.Bacc("TRN2", target_bir_lowering=False, num_devices=1)
    args = [nc.dram_tensor(f"in_{k}", v.shape, mybir.dt.from_np(v.dtype), kind="ExternalInput").ap()
            for k, v in arrays.items()]
    out = nc.dram_tensor("out", _OUTS[0][0], FP32, kind="ExternalOutput").ap()
    program(nc, *args, out.rearrange("b c t -> (b c) t"))
    r = _run(nc, [{f"in_{k}": v for k, v in arrays.items()}], core_ids=[0])
    return r.results[0]["out"]
```

```python
import numpy as np
import concourse.bass as bass
from concourse import mybir
from contextlib import ExitStack

FP32 = mybir.dt.float32
F32R = mybir.dt.float32r
F16 = mybir.dt.float16
I32 = mybir.dt.int32
ALU = mybir.AluOpType
ACT = mybir.ActivationFunctionType
AX = mybir.AxisListType
MAX_OP = bass.bass_isa.ReduceOp.max
ADD_OP = bass.bass_isa.ReduceOp.add

B, CH, T = 64, 32, 512
P = 128
GB = P // CH
NG = B // GB
NT = T // P
STEPS = GB * NT
DMA = 16
START = 1
TOK_SCALE = float(np.float32(1.0 / np.sqrt(np.sqrt(32.0)))) ** 2


D = 512
KD = D // P
HEADS, KV, HD = 16, 4, 128
FF = 1408
Q_AT, K_AT, V_AT, O_AT = 0, KD * HEADS * HD, KD * (HEADS + KV) * HD, KD * (HEADS + 2 * KV) * HD
ATTN_W = O_AT + HEADS * D
FFN_W = 3 * KD * FF
ATTN_PARTS = ((Q_AT, K_AT), (K_AT, V_AT), (V_AT, O_AT), (O_AT, ATTN_W))
A_CHUNK, F_CHUNK = 1024, FF
A_CHUNKS, F_CHUNKS = ATTN_W // A_CHUNK, FFN_W // F_CHUNK
LN_EPS, RMS_EPS, GAMMA_EPS = 1e-5, 1e-6, 1e-8
X_SCALE = 2.0 ** 11


class Weights:

    def __init__(self, sb):
        self.a_hi, self.a_lo = sb("attn_hi", [P, ATTN_W], F16), sb("attn_lo", [P, ATTN_W], F16)
        self.scale = sb("w_scale", [P, 4])
        self.eps_q, self.eps_k = sb("eps_q", [P, 1]), sb("eps_k", [P, 1])
        self.o_unscale = sb("o_unscale", [P, 1])


def token_attention(nc, x, vt, h1, ident_in, W, w_attn, w_ffn, ffn_store):
    with ExitStack() as ctx:
        def sb(name, shape, dt=FP32):
            return ctx.enter_context(nc.sbuf_tensor(name, shape, dt))

        def pb(name):
            return ctx.enter_context(nc.psum_tensor(name, [P, T], FP32))

        def sem(name):
            return ctx.enter_context(nc.semaphore(name))

        NB = 3
        QP = [sb(f"q_parts{n}", [P, GB, T], F32R) for n in range(NB)]
        KP = [sb(f"k_parts{n}", [P, GB, T], F32R) for n in range(NB)]
        VT = [sb(f"v_t{n}", [P, NT, P]) for n in range(NB)]
        q_raw = sb("q_raw", [P, GB, T])
        k_raw = sb("k_raw", [P, GB, T])
        NE = 3 * GB
        E = sb("exps", [P, NE, T])
        ident = sb("tok_ident", [P, P])
        ones = sb("tok_ones", [P, CH])
        row_max = sb("row_max", [P, NB, STEPS])
        max_parts = sb("max_parts", [P, 2, STEPS], F32R)
        max_t = sb("max_t", [2 * STEPS, P])
        h_tile = sb("h_tile", [P, T])
        den = sb("tok_den_sum", [P, T])
        rden = sb("tok_rden", [P, NT, GB])
        out = sb("tok_out_sum", [P, T])

        raw_a = [sb(f"raw_attn{n}", [P, A_CHUNK]) for n in range(2)]
        raw_f = [sb(f"raw_ffn{n}", [P, F_CHUNK]) for n in range(2)]
        ternary = [sb(f"ternary{n}", [P, F_CHUNK], F16) for n in range(2)]
        amax, fsum = sb("w_amax", [P, A_CHUNKS]), sb("w_fsum", [P, F_CHUNKS])
        amax4, amax_all = sb("w_amax4", [P, 4]), sb("w_amax_all", [P, 4])
        fsum3, fsum_all = sb("w_fsum3", [P, 3]), sb("w_fsum_all", [P, 3])
        tmp, pow2 = sb("w_tmp", [P, 4]), sb("w_pow2", [P, 4])
        scale_of = sb("w_scale_of", [P, A_CHUNKS])
        thr_of, nthr_of = sb("w_thr_of", [P, F_CHUNKS]), sb("w_nthr_of", [P, F_CHUNKS])

        S = [pb(f"score_rows{n}") for n in range(2)]
        ST = [pb(f"score_cols{n}") for n in range(3)]
        OUT = pb("tok_out")
        DEN = pb("tok_den")
        MT = pb("max_transposed")

        ident_in_sem = sem("t_ident_in")
        const_set = sem("t_const_set")
        q_in, k_in = sem("t_q_in"), sem("t_k_in")
        v_in = [sem(f"t_v_in{n}") for n in range(NB)]
        hi_done, q_lo, k_lo = sem("t_hi_done"), sem("t_q_lo"), sem("t_k_lo")
        s_done, max_done, max_split = sem("t_s_done"), sem("t_max_done"), sem("t_max_split")
        mt_done, mt_out, max_in = sem("t_mt_done"), sem("t_mt_out"), sem("t_max_in")
        st_done, exp_done, pv_done = sem("t_st_done"), sem("t_exp_done"), sem("t_pv_done")
        picked, rden_done, spread = sem("t_picked"), sem("t_rden_done"), sem("t_spread")
        sums_out, h_done, h_out = sem("t_sums_out"), sem("t_h_done"), sem("t_h_out")
        a_in = [sem(f"w_a_in{n}") for n in range(2)]
        f_in = [sem(f"w_f_in{n}") for n in range(2)]
        a_stat, f_stat = sem("w_a_stat"), sem("w_f_stat")
        folded, reduced, chain = sem("w_folded"), sem("w_reduced"), sem("w_chain")
        a_hi, a_lo = sem("w_a_hi"), sem("w_a_lo")
        f_below, f_done, f_stored = sem("w_f_below"), sem("w_f_done"), sem("w_f_stored")
        EXP_CREDIT = 3
        PV_CREDIT = 3

        AHEAD = 6
        TAKE = 1
        MAX_AT = 2 + STEPS - AHEAD
        PICK_AT, SPREAD_AT = 4, 5
        VALUES_AT = [7, 9, 10, 11, 13, 15, 16, 17]
        SPLIT_AT = [2, 3, 4, 5]
        MEASURE_AT, CONVERT_AT = [12, 16], [11, 16]
        PEEL = NG - 4
        MEASURED = 6
        A_MEASURED = (4, 4, 2)
        A_ROUND = sum(A_MEASURED)
        SCALED = 14
        block = ctx.enter_context(nc.Block())

        def measure(j, p):
            return {"measure": True, "round": j, "a": A_ROUND * j + 4 * p, "a_count": A_MEASURED[p],
                    "f": 2 * (NB * j + p), "f_count": 2}

        def convert(g, j):
            i = g - MEASURED
            f, f_count = i, 1
            if isinstance(g, int):
                f, f_count = i + g - PEEL, 2 if g + 1 < NG else 0
            return {"measure": False, "round": j, "i": i, "a": 2 * i, "a_count": 2, "f": f, "f_count": f_count}

        def over_groups(eng, body, scales=None):
            with eng.Fori(0, MEASURED // NB) as j:
                for p in range(NB):
                    body(j * NB + p, p, True, True, measure(j, p))
            if scales:
                scales()
            with eng.Fori(MEASURED // NB, PEEL // NB) as j:
                for p in range(NB):
                    body(j * NB + p, p, True, True, convert(j * NB + p, j))
            for g in range(PEEL, NG):
                body(g, g % NB, g + 1 < NG, g + 2 < NG, convert(g, g // NB))

        @block.sync
        def _(sp):
            def load_qk(g):
                for raw, lo, done, first in ((q_raw, q_lo, q_in, 0), (k_raw, k_lo, k_in, CH)):
                    sp.wait_ge(lo, g)
                    for r in range(3):
                        sp.dma_start(raw[r * CH:(r + 1) * CH, :, :],
                                     x[bass.ds(g * GB, GB), first:first + CH, :].rearrange("b c t -> c b t")
                                     ).then_inc(done, DMA)

            def load_v(g, p):
                sp.dma_start(VT[p][:, :, :], vt[bass.ds(g, 1), :, :].rearrange("g s n -> (g s) n")
                             ).then_inc(v_in[p], DMA)

            def store_max(g, p):
                sp.wait_ge(mt_out, g + 1)
                for part in range(2):
                    row = QP[p][3 * CH + part:3 * CH + part + 1, :, :].bitcast(FP32)
                    sp.dma_start(row,
                                 max_t[part * STEPS:(part + 1) * STEPS, :]).then_inc(max_in, DMA)

            def load_attn(a, first):
                for n in range(2):
                    sp.wait_ge(a_stat, a + first + n + 1)
                    sp.dma_start(raw_a[n][:, :], w_attn[:, bass.ds((a + first + n) * A_CHUNK, A_CHUNK)]
                                 ).then_inc(a_in[n], DMA)

            def convert_attn(c, n):
                sp.dma_start(raw_a[n][:, :], w_attn[:, bass.ds(c * A_CHUNK, A_CHUNK)]).then_inc(a_in[n], DMA)

            sp.dma_start(ident[:, :], ident_in).then_inc(ident_in_sem, DMA)
            load_qk(0)
            load_v(0, 0)
            load_qk(1)
            load_v(1, 1)
            load_qk(2)
            store_max(0, 0)

            def body(g, p, more, more2, w):
                for n in range(w["f_count"]):
                    if w["measure"]:
                        sp.wait_ge(f_stat, w["f"] + START)
                    sp.dma_start(raw_f[n][:, :], w_ffn[:, bass.ds((w["f"] + n) * F_CHUNK, F_CHUNK)]
                                 ).then_inc(f_in[n], DMA)
                if w["measure"]:
                    load_attn(w["a"], 0)
                else:
                    sp.wait_ge(a_lo, w["a"] + START)
                    convert_attn(w["a"] + 1, 1)
                if more2:
                    sp.wait_ge(pv_done, NT * g + PV_CREDIT)
                    load_v(g + 2, (p + 2) % NB)
                if more:
                    store_max(g + 1, (p + 1) % NB)
                if more2 and not (isinstance(g, int) and g + 3 >= NG):
                    load_qk(g + 3)
                if w["measure"] and w["a_count"] > 2:
                    load_attn(w["a"], 2)
                if not w["measure"] and not (isinstance(w["a"], int) and w["a"] + 2 >= A_CHUNKS):
                    sp.wait_ge(a_lo, w["a"] + 1 + START)
                    convert_attn(w["a"] + 2, 0)
                if not w["measure"]:
                    sp.wait_ge(f_done, w["f"] + w["f_count"])
                sp.wait_ge(h_done, g + 1 + START)
                sp.dma_start(h1[bass.ds(g * P, P), :], h_tile[:, :]).then_inc(h_out, DMA)
                if not w["measure"]:
                    for n in range(w["f_count"]):
                        sp.dma_start(ffn_store[:, bass.ds((w["f"] + n) * F_CHUNK, F_CHUNK)], ternary[n][:, :]
                                     ).then_inc(f_stored, DMA)

            def measured():
                sp.wait_ge(a_stat, A_CHUNKS + 2)
                sp.wait_ge(f_stat, F_CHUNKS + START)
                convert_attn(0, 0)

            over_groups(sp, body, measured)
            sp.wait_ge(f_stored, F_CHUNKS * DMA + START)
            sp.wait_ge(h_out, NG * DMA + START)

        @block.gpsimd
        def _(pool):
            def split_q_lo(g, p):
                pool.wait_ge(hi_done, 4 * g + 2)
                nc.gpsimd.tensor_tensor(QP[p][CH:2 * CH, :, :], q_raw[CH:2 * CH, :, :],
                                        QP[p][CH:2 * CH, :, :].bitcast(FP32), ALU.subtract).then_inc(q_lo, 1)

            def split_k_lo(g, p):
                pool.wait_ge(hi_done, 4 * g + 4)
                nc.gpsimd.tensor_tensor(KP[p][2 * CH:3 * CH, :, :], k_raw[2 * CH:3 * CH, :, :],
                                        KP[p][2 * CH:3 * CH, :, :].bitcast(FP32), ALU.subtract).then_inc(k_lo, 1)

            split_q_lo(0, 0)
            split_q_lo(1, 1)
            split_k_lo(1, 1)

            def body(g, p, more, more2, w):
                if more2:
                    split_q_lo(g + 2, (p + 2) % NB)
                    split_k_lo(g + 2, (p + 2) % NB)

            def reduce_partitions():
                pool.wait_ge(folded, 4 + 3)
                nc.gpsimd.partition_all_reduce(amax_all[:, :], amax4[:, :], P, MAX_OP).then_inc(reduced, 1)
                pool.wait_ge(reduced, 1)
                nc.gpsimd.partition_all_reduce(fsum_all[:, :], fsum3[:, :], P, ADD_OP).then_inc(reduced, 1)
                pool.wait_ge(reduced, 2)

            over_groups(pool, body, reduce_partitions)

        @block.scalar
        def _(act):
            def split_hi(g, p, n):
                raw, parts, done = ((q_raw, QP[p], q_in), (k_raw, KP[p], k_in))[n // 2]
                two = slice(2 * (n % 2), 2 * (n % 2) + 2)
                if n % 2 == 0:
                    act.wait_ge(done, 3 * DMA * (g + 1))
                nc.scalar.copy(parts[0:3 * CH, two, :], raw[0:3 * CH, two, :]).then_inc(hi_done, 1)

            for g in range(2):
                for n in range(4):
                    split_hi(g, g, n)

            def exps(g, p, u):
                act.wait_ge(st_done, STEPS * g + u + 1)
                if u % GB == 0:
                    act.wait_ge(pv_done, NT * g + u // GB - 2 + PV_CREDIT)
                nc.scalar.activation(E[:, (STEPS * p + u) % NE, :], ST[(p + u) % 3][:, :], ACT.Exp,
                                     scale=TOK_SCALE).then_inc(exp_done, 1)

            act.sem_inc(sums_out, START)
            act.wait_ge(pv_done, PV_CREDIT)
            exps(0, 0, 0)
            exps(0, 0, 1)

            def body(g, p, more, more2, w):
                for u in range(2, STEPS + 2):
                    if more2 and u in SPLIT_AT:
                        split_hi(g + 2, (p + 2) % NB, SPLIT_AT.index(u))
                    if u < STEPS:
                        exps(g, p, u)
                    elif more:
                        exps(g + 1, (p + 1) % NB, u - STEPS)
                    at = MEASURE_AT if w["measure"] else CONVERT_AT
                    if u in at:
                        n = at.index(u)
                        if w["measure"]:
                            act.wait_ge(f_in[n], DMA * (g + 1))
                            act.wait_ge(f_stat, w["f"] + START)
                            nc.scalar.activation(ternary[n][:, :], raw_f[n][:, :], ACT.Abs,
                                                 accum_out=fsum[:, bass.ds(w["f"] + n, 1)]).then_inc(f_stat, 1)
                        else:
                            act.wait_ge(chain, SCALED)
                            act.wait_ge(a_in[n], DMA * (A_CHUNKS // 2 + w["i"] + 1))
                            nc.scalar.activation(W.a_hi[:, bass.ds((w["a"] + n) * A_CHUNK, A_CHUNK)], raw_a[n][:, :],
                                                 ACT.Copy, scale=scale_of[:, bass.ds(w["a"] + n, 1)]).then_inc(a_hi, 1)
                act.wait_ge(pv_done, NT * (g + 1) + PV_CREDIT)
                act.wait_ge(h_done, g + START)
                nc.scalar.copy(den[:, :], DEN[:, :]).then_inc(sums_out, 1)
                nc.scalar.copy(out[:, :], OUT[:, :]).then_inc(sums_out, 1)

            over_groups(act, body)

        @block.vector
        def _(dve):
            def maximum(g, p, k):
                dve.wait_ge(s_done, STEPS * g + k + 1)
                nc.vector.reduce_max(row_max[:, p, k:k + 1], S[k % 2][:, :], AX.X).then_inc(max_done, 1)

            def split_maxima(g, p):
                dve.wait_ge(max_done, STEPS * (g + 1))
                nc.vector.tensor_scalar(max_parts[:, 0, :], row_max[:, p, :], -1.0, None, ALU.mult
                                        ).then_inc(max_split, 1)
                dve.wait_ge(max_split, 2 * g + 1)
                nc.vector.scalar_tensor_tensor(max_parts[:, 1, :], row_max[:, p, :], -1.0,
                                               max_parts[:, 0, :].bitcast(FP32), ALU.mult, ALU.subtract
                                               ).then_inc(max_split, 1)

            def take_transposed(g):
                dve.wait_ge(mt_done, g + 1)
                dve.wait_ge(max_in, 2 * DMA * g)
                nc.vector.tensor_copy(max_t[:, :], MT[0:2 * STEPS, 0:P]).then_inc(mt_out, 1)

            nc.vector.memset(ones[:, :], 1.0).then_inc(const_set, 1)
            for n in range(NB):
                nc.vector.memset(KP[n][3 * CH:3 * CH + 2, :, :].bitcast(FP32), 1.0).then_inc(const_set, 1)
            dve.sem_inc(h_done, START)
            dve.sem_inc(h_out, START)
            for start, count in ((a_stat, 2), (f_stat, START), (a_lo, START), (f_stored, START)):
                dve.sem_inc(start, count)

            def largest(w, i):
                if i < w["a_count"]:
                    dve.wait_ge(a_in[i % 2], (DMA // 2) * (w["a"] + 2 * (i // 2)) + DMA)
                    nc.vector.tensor_reduce(amax[:, bass.ds(w["a"] + i, 1)], raw_a[i % 2][:, :], AX.X, ALU.max,
                                            apply_absolute_value=True).then_inc(a_stat, 1)

            def below(g, w, n):
                if n < w["f_count"]:
                    seen = g - (PEEL if n else 0)
                    dve.wait_ge(f_in[n], DMA * (g + 1) if n == 0 else DMA * (MEASURED + seen + 1))
                    dve.wait_ge(f_stored, DMA * w["f"] + START)
                    nc.vector.tensor_scalar(ternary[n][:, :], raw_f[n][:, :], nthr_of[:, bass.ds(w["f"] + n, 1)], None,
                                            ALU.is_lt).then_inc(f_below, 1)

            def above(g, w, n):
                if n < w["f_count"]:
                    dve.wait_ge(f_below, w["f"] + n + 1)
                    nc.vector.scalar_tensor_tensor(ternary[n][:, :], raw_f[n][:, :], thr_of[:, bass.ds(w["f"] + n, 1)],
                                                   ternary[n][:, :], ALU.is_gt, ALU.subtract).then_inc(f_done, 1)

            def low(w, n):
                dve.wait_ge(a_hi, w["a"] + n + 1)
                at = bass.ds((w["a"] + n) * A_CHUNK, A_CHUNK)
                nc.vector.scalar_tensor_tensor(W.a_lo[:, at], raw_a[n][:, :], scale_of[:, bass.ds(w["a"] + n, 1)],
                                               W.a_hi[:, at], ALU.mult, ALU.subtract).then_inc(a_lo, 1)

            def weights(g, w, i):
                if w["measure"]:
                    largest(w, i)
                elif i == 0:
                    below(g, w, 0)
                elif i == 1:
                    above(g, w, 0)
                else:
                    low(w, i - 2)
                    (below, above)[i - 2](g, w, 1)

            def finish(g):
                dve.wait_ge(spread, g + 1)
                dve.wait_ge(sums_out, 2 * g + 2 + START)
                dve.wait_ge(h_out, DMA * g + START)
                nc.vector.tensor_tensor(h_tile[:, :], out[:, :], DEN[:, :], ALU.mult).then_inc(h_done, 1)


            def scales():
                dve.wait_ge(a_stat, A_CHUNKS + 2)
                dve.wait_ge(f_stat, F_CHUNKS + START)
                for m, (lo, hi) in enumerate(ATTN_PARTS):
                    nc.vector.tensor_reduce(amax4[:, m:m + 1], amax[:, lo // A_CHUNK:hi // A_CHUNK], AX.X, ALU.max
                                            ).then_inc(folded, 1)
                for m in range(3):
                    nc.vector.tensor_reduce(fsum3[:, m:m + 1], fsum[:, m * KD:(m + 1) * KD], AX.X, ALU.add
                                            ).then_inc(folded, 1)
                steps = [0]

                def link(ins):
                    steps[0] += 1
                    ins.then_inc(chain, 1)
                    dve.wait_ge(chain, steps[0])

                dve.wait_ge(reduced, 2)
                link(nc.vector.tensor_scalar(tmp[:, :], amax_all[:, :], 1e-30, None, ALU.max))
                link(nc.vector.tensor_scalar(pow2[:, :].bitcast(I32), tmp[:, :].bitcast(I32), 0x7f800000, None,
                                             ALU.bitwise_and))
                link(nc.vector.reciprocal(tmp[:, :], pow2[:, :]))
                link(nc.vector.tensor_scalar(W.scale[:, :], tmp[:, :], 2.0 ** 10, None, ALU.mult))
                link(nc.vector.tensor_tensor(tmp[:, :], W.scale[:, :], W.scale[:, :], ALU.mult))
                link(nc.vector.tensor_scalar(W.eps_q[:, :], tmp[:, 0:1], HD * RMS_EPS * X_SCALE ** 2, None, ALU.mult))
                link(nc.vector.tensor_scalar(W.eps_k[:, :], tmp[:, 1:2], RMS_EPS * X_SCALE ** 2, None, ALU.mult))
                link(nc.vector.tensor_tensor(tmp[:, 0:1], pow2[:, 2:3], pow2[:, 3:4], ALU.mult))
                link(nc.vector.tensor_scalar(W.o_unscale[:, :], tmp[:, 0:1], 2.0 ** -15, None, ALU.mult))
                for m, (lo, hi) in enumerate(ATTN_PARTS):
                    n = (hi - lo) // A_CHUNK
                    last = nc.vector.tensor_copy(scale_of[:, lo // A_CHUNK:hi // A_CHUNK],
                                                 W.scale[:, m:m + 1].to_broadcast([P, n]))
                link(last)
                link(nc.vector.tensor_scalar(tmp[:, 0:3], fsum_all[:, :], 1.0 / (FF * D), GAMMA_EPS, ALU.mult, ALU.add))
                for m in range(3):
                    of = slice(m * KD, (m + 1) * KD)
                    mean = tmp[:, m:m + 1].to_broadcast([P, KD])
                    link(nc.vector.tensor_scalar(thr_of[:, of], mean, 0.5, None, ALU.mult))
                    last = nc.vector.tensor_scalar(nthr_of[:, of], mean, -0.5, None, ALU.mult)
                link(last)

            dve.wait_ge(hi_done, 4)
            nc.vector.tensor_tensor(KP[0][2 * CH:3 * CH, :, :], k_raw[2 * CH:3 * CH, :, :],
                                    KP[0][2 * CH:3 * CH, :, :].bitcast(FP32), ALU.subtract).then_inc(k_lo, 1)
            for k in range(STEPS):
                maximum(0, 0, k)
            split_maxima(0, 0)
            take_transposed(0)
            PIECES_AT = [1, 3, 9, 11]
            INVERT_AT, FINISH_AT = 8, 9
            EARLY = 14
            for k in range(EARLY):
                maximum(1, 1, k)

            def body(g, p, more, more2, w):
                if more:
                    for k in range(EARLY, STEPS):
                        maximum(g + 1, (p + 1) % NB, k)
                    split_maxima(g + 1, (p + 1) % NB)
                    if not more2:
                        take_transposed(g + 1)
                if more2:
                    for k in range(AHEAD):
                        maximum(g + 2, (p + 2) % NB, k)
                        if k == TAKE:
                            take_transposed(g + 1)
                        if k in PIECES_AT:
                            weights(g, w, PIECES_AT.index(k))
                else:
                    for n in range(2):
                        weights(g, w, n)
                def invert():
                    dve.wait_ge(picked, g + 1)
                    nc.vector.reciprocal(rden[:, :, :].rearrange("p i b -> p (i b)"), MT[:, P:P + STEPS]
                                         ).then_inc(rden_done, 1)

                for k in range(AHEAD, EARLY):
                    if more2:
                        maximum(g + 2, (p + 2) % NB, k)
                    if k in PIECES_AT:
                        weights(g, w, PIECES_AT.index(k))
                    if k == INVERT_AT:
                        invert()
                    if k == FINISH_AT:
                        finish(g)

            over_groups(dve, body, scales)

        @block.tensor
        def _(pe):
            def rows(g, p, k):
                b, t = k // NT, k % NT
                if k == 0:
                    pe.wait_ge(q_lo, g + 1)
                    pe.wait_ge(k_lo, g + 1)
                if not (isinstance(g, int) and STEPS * g + k < 2):
                    pe.wait_ge(max_done, STEPS * g + k - 1)
                nc.tensor.matmul(S[k % 2][:, :], QP[p][0:3 * CH, b, t * P:(t + 1) * P], KP[p][0:3 * CH, b, :],
                                 start=True, stop=True).then_inc(s_done, 1)

            def transpose_maxima(g):
                pe.wait_ge(max_split, 2 * (g + 1))
                pe.wait_ge(mt_out, g)
                nc.tensor.matmul(MT[0:2 * STEPS, 0:P], max_parts[:, :, :].bitcast(FP32), ident[:, :],
                                 start=True, stop=True).then_inc(mt_done, 1)

            def cols(g, p, u):
                i, b = u // GB, u % GB
                if u == 0:
                    pe.wait_ge(max_in, 2 * DMA * (g + 1))
                pe.wait_ge(exp_done, STEPS * g + u - 2 + EXP_CREDIT)
                nc.tensor.matmul(ST[(p + u) % 3][:, :], KP[p][0:3 * CH + 2, b, i * P:(i + 1) * P],
                                 QP[p][0:3 * CH + 2, b, :], start=True, stop=True).then_inc(st_done, 1)

            def values(g, p, w, i, sums):
                if i == 0 and sums:
                    pe.wait_ge(h_done, g + START)
                if i == 0 and not sums:
                    pe.wait_ge(sums_out, 2 * g + START)
                    pe.wait_ge(v_in[p], DMA * (w["round"] + 1))
                pe.wait_ge(exp_done, STEPS * g + GB * (i + 1) + EXP_CREDIT)
                for b in range(GB):
                    into, by = (DEN, ones[:, :]) if sums else (OUT, VT[p][:, i, b * CH:(b + 1) * CH])
                    last = nc.tensor.matmul(into[b * CH:(b + 1) * CH, :], by, E[:, (STEPS * p + GB * i + b) % NE, :],
                                            start=(i == 0), stop=(i == NT - 1))
                if sums:
                    last.then_inc(pv_done, 1)

            pe.wait_ge(ident_in_sem, DMA)
            pe.wait_ge(const_set, 1 + NB)
            for _ in range(EXP_CREDIT):
                pe.sem_inc(exp_done, 1)
            for _ in range(PV_CREDIT):
                pe.sem_inc(pv_done, 1)
            for k in range(STEPS):
                rows(0, 0, k)
            transpose_maxima(0)
            for k in range(AHEAD):
                rows(1, 1, k)
            cols(0, 0, 0)
            cols(0, 0, 1)

            def pick(g):
                pe.wait_ge(sums_out, 2 * g + 1 + START)
                first = ident[:, :].rearrange("p (b c) -> p b c", c=CH)[:, :, 0]
                for i in range(NT):
                    last = nc.tensor.matmul(MT[:, P + i * GB:P + (i + 1) * GB], den[:, i * P:(i + 1) * P], first,
                                            start=True, stop=True)
                last.then_inc(picked, 1)

            def spread_inverses(g):
                pe.wait_ge(rden_done, g + 1)
                for i in range(NT):
                    for b in range(GB):
                        last = nc.tensor.matmul(DEN[b * CH:(b + 1) * CH, i * P:(i + 1) * P],
                                                rden[:, i, b:b + 1].to_broadcast([P, CH]), ident[:, :],
                                                start=True, stop=True)
                last.then_inc(spread, 1)

            def step(g, p, u, more, more2, w):
                q = (p + 1) % NB
                if u < MAX_AT and more:
                    rows(g + 1, q, u - 2 + AHEAD)
                if u >= MAX_AT and more2:
                    rows(g + 2, (p + 2) % NB, u - MAX_AT)
                if more and u == MAX_AT + TAKE:
                    transpose_maxima(g + 1)
                if u < STEPS:
                    cols(g, p, u)
                elif more:
                    cols(g + 1, q, u - STEPS)
                if u in VALUES_AT:
                    values(g, p, w, *divmod(VALUES_AT.index(u), 2))

            def body(g, p, more, more2, w):
                for u in range(SPREAD_AT + 1, STEPS + 2):
                    step(g, p, u, more, more2, w)
                for u in range(2, SPREAD_AT + 1):
                    if more:
                        step(g + 1, (p + 1) % NB, u, more2, not isinstance(g, int) or g + 3 < NG, None)
                    if u == PICK_AT:
                        pick(g)
                    if u == SPREAD_AT:
                        spread_inverses(g)

            for u in range(2, SPREAD_AT + 1):
                step(0, 0, u, True, True, None)
            over_groups(pe, body)


TOK = 64 * 32
NTT = TOK // P
SEQ = 32
BT = P // SEQ
G = HEADS // KV
KF = FF // P
V_SHIFT = 2.0 ** -16


def blocks(nc, W, ffn_store, h1, tables_in, norm_in, mask_in, block_in, ident_in, out):
    with ExitStack() as ctx:
        def sb(name, shape, dt=FP32):
            return ctx.enter_context(nc.sbuf_tensor(name, shape, dt))

        def sem(name):
            return ctx.enter_context(nc.semaphore(name))

        PROJ = [ctx.enter_context(nc.psum_tensor(f"proj{n}", [P, D], FP32)) for n in range(2)]
        TR = [ctx.enter_context(nc.psum_tensor(f"transposed{n}", [P, D], FP32)) for n in range(2)]
        FB = [ctx.enter_context(nc.psum_tensor(f"ffn_sum{n}", [P, D], FP32)) for n in range(4)]
        PV_BANK = [FB[0], FB[1], FB[3], FB[0]]
        SCORES = FB[2]

        ffn_w = sb("ffn_w", [P, FFN_W], F16)
        tables = sb("tables", [P, 4, HD])
        norm_w = sb("norm_w", [P, 4, HD])
        mask = sb("mask", [P, SEQ])
        own = sb("own_batch", [P, BT])
        ident = sb("ident", [P, P])
        minus_half = sb("minus_half", [P, HEADS])
        h_ln = sb("h_ln", [P, D])
        h_res = sb("h_res", [P, D])
        stats = sb("stats", [P, 2, 6])
        mv = sb("mv", [P, 2, 2])
        var = sb("var", [P, 2, 1])
        rstd = sb("rstd", [P, 2, 1])
        xn = sb("xn", [P, D])
        xh, xl = sb("x_hi", [P, D], F16), sb("x_lo", [P, D], F16)
        sq = [sb(f"squares{n}", [P, D]) for n in range(2)]
        ss = sb("sums_sq", [P, KV + HEADS])
        ms = sb("mean_sq", [P, KV + HEADS])
        rr = sb("rms_inv", [P, KV + HEADS])
        ra = [sb(f"rope_cos{n}", [P, D]) for n in range(2)]
        rb = [sb(f"rope_sin{n}", [P, D]) for n in range(2)]
        rope = sb("roped", [P, 1 + KV, D])
        kT = sb("k_t", [P, KV, P])
        qT = sb("q_t", [P, KV, G * P])
        v = sb("v", [P, KV * HD])
        sm = sb("scores", [P, HEADS, SEQ])
        sd = sb("scores_less_max", [P, HEADS, SEQ])
        pr = sb("probs", [P, HEADS, SEQ])
        mx = sb("row_maxima", [P, HEADS])
        den = sb("row_sums", [P, HEADS])
        rden = sb("row_sums_inv", [P, HEADS])
        pbd = sb("probs_blocks", [P, KV, BT, G * SEQ])
        ch, cl = sb("ctx_hi", [P, HEADS, P], F16), sb("ctx_lo", [P, HEADS, P], F16)
        h2 = sb("h2", [P, D])
        x2n = sb("x2n", [P, D])
        x2h, x2l = sb("x2_hi", [P, D], F16), sb("x2_lo", [P, D], F16)
        th = sb("tanh", [P, D])
        hid = sb("hidden", [P, D])
        hh, hl = sb("hidden_hi", [P, KF, P], F16), sb("hidden_lo", [P, KF, P], F16)
        o_tile = sb("out_tile", [P, D])

        const_in, const_set = sem("b_const_in"), sem("b_const_set")
        ffn_in = sem("b_ffn_in")
        ln_in, res_in, out_done = sem("b_ln_in"), sem("b_res_in"), sem("b_out_done")
        ln1_var, ln1_rstd, ln1 = sem("b_ln1_var"), sem("b_ln1_rstd"), sem("b_ln1")
        ln2_var, ln2_rstd, ln2 = sem("b_ln2_var"), sem("b_ln2_rstd"), sem("b_ln2")
        xt, x_hi, x_lo = sem("b_xt"), sem("b_x_hi"), sem("b_x_lo")
        proj, squared, ssum, roped_a, roped_b = (sem("b_proj"), sem("b_squared"), sem("b_ssum"), sem("b_roped_a"),
                                                 sem("b_roped_b"))
        added, mean_sq, rms, q_ready, v_out = (sem("b_added"), sem("b_mean_sq"), sem("b_rms"), sem("b_q_ready"),
                                               sem("b_v_out"))
        qkt, qkt_out = sem("b_qkt"), sem("b_qkt_out")
        scored, masked, sub, exped, probs = (sem("b_scored"), sem("b_masked"), sem("b_sub"), sem("b_exped"),
                                             sem("b_probs"))
        soft = sem("b_soft")
        ln1_self, ln2_self = sem("b_ln1_self"), sem("b_ln2_self")
        pt, pbd_out, pv, c_hi, c_lo = sem("b_pt"), sem("b_pbd_out"), sem("b_pv"), sem("b_c_hi"), sem("b_c_lo")
        o_sum, h2_done = sem("b_o_sum"), sem("b_h2_done")
        xt2, x2_hi, x2_lo = sem("b_xt2"), sem("b_x2_hi"), sem("b_x2_lo")
        f1, tanhed, gated, hid_hi, hid_lo = (sem("b_f1"), sem("b_tanhed"), sem("b_gated"), sem("b_hid_hi"),
                                             sem("b_hid_lo"))
        w3, o_out = sem("b_w3"), sem("b_o_out")

        NPROJ = 2 + KV
        FG = [range(0, 4), range(4, 8), range(8, KF)]
        NF = len(FG)
        TRANSPOSE_AT = {(0, 0): [0], (0, 1): [1], (1, 0): [2, 3], (1, 1): [4]}
        SCORES_AT = (2, 0)
        DOWN_FIRST = 8
        block = ctx.enter_context(nc.Block())

        def over_tiles(eng, body):
            body(0, True, False)
            with eng.Fori(1, NTT - 1) as n:
                body(n, True, True)
            body(NTT - 1, True, True)
            body(NTT, False, True)

        def bcast(ap, shape, at):
            return ap.unsqueeze(at).to_broadcast(shape)

        @block.sync
        def _(sp):
            sp.dma_start(h_ln[:, :], h1[0:P, :]).then_inc(ln_in, DMA)
            for dst, src in ((tables[:, :, :], tables_in), (norm_w[:, :, :], norm_in), (mask[:, :], mask_in),
                             (own[:, :], block_in), (ident[:, :], ident_in)):
                sp.dma_start(dst, src).then_inc(const_in, DMA)
            for m in range(3):
                of = slice(m * KD * FF, (m + 1) * KD * FF)
                sp.dma_start(ffn_w[:, of], ffn_store[:, of]).then_inc(ffn_in, DMA)

            def body(n, attn, ffn):
                if attn and not (isinstance(n, int) and n + 1 >= NTT):
                    sp.wait_ge(ln1, n + 1)
                    sp.dma_start(h_ln[:, :], h1[bass.ds((n + 1) * P, P), :]).then_inc(ln_in, DMA)
                if attn:
                    sp.wait_ge(h2_done, n)
                    sp.dma_start(h_res[:, :], h1[bass.ds(n * P, P), :]).then_inc(res_in, DMA)
                if ffn:
                    sp.wait_ge(o_out, n + START)
                    sp.dma_start(out[bass.ds((n - 1) * P, P), :], o_tile[:, :]).then_inc(out_done, DMA)

            over_tiles(sp, body)
            sp.wait_ge(out_done, DMA * NTT + START)

        @block.gpsimd
        def _(pool):
            def inv_std(n, m, var_done, out_sem):
                pool.wait_ge(var_done, n + 1)
                nc.gpsimd.tensor_tensor(rstd[:, m, :], var[:, m, :], minus_half[:, 0:1], ALU.pow).then_inc(out_sem, 1)

            pool.wait_ge(const_set, 1)
            inv_std(0, 0, ln1_var, ln1_rstd)

            def body(n, attn, ffn):
                if not attn:
                    return

                def add_parts(c):
                    pool.wait_ge(roped_b, 5 * n + c + 1)
                    nc.gpsimd.tensor_tensor(rope[:, c, :], ra[c % 2][:, :], rb[c % 2][:, :], ALU.add
                                            ).then_inc(added, 1)

                def invert(c):
                    pool.wait_ge(mean_sq, 5 * n + c + 1)
                    of = slice(G * c, G * c + G)
                    nc.gpsimd.tensor_tensor(rr[:, of], ms[:, of], minus_half[:, 0:G], ALU.pow).then_inc(rms, 1)

                def normalise(c):
                    pool.wait_ge(added, 5 * n + c + 1)
                    pool.wait_ge(rms, 5 * n + c + 1)
                    view = rope[:, c, :].rearrange("p (h d) -> p h d", d=HD)
                    nc.gpsimd.tensor_tensor(view, view, bcast(rr[:, G * c:G * c + G], [P, G, HD], 2), ALU.mult
                                            ).then_inc(q_ready, 1)

                for c in range(1 + KV):
                    add_parts(c)
                    invert(c)
                    normalise(c)
                if not (isinstance(n, int) and n + 1 >= NTT):
                    inv_std(n + 1, 0, ln1_var, ln1_rstd)
                inv_std(n, 1, ln2_var, ln2_rstd)

            over_tiles(pool, body)

        @block.scalar
        def _(act):
            def take_x(n):
                act.wait_ge(xt, n + 1)
                nc.scalar.copy(xh[:, :], TR[0][:, :]).then_inc(x_hi, 1)

            def square(n, c):
                act.wait_ge(proj, NPROJ * n + c + 1)
                if not (isinstance(n, int) and 5 * n + c < 2):
                    act.wait_ge(ssum, 5 * n + c - 1)
                nc.scalar.activation(sq[c % 2][:, :], PROJ[c % 2][:, :], ACT.Square).then_inc(squared, 1)

            def tanh(n, f):
                w = len(FG[f]) * P
                act.wait_ge(f1, 2 * NF * n + 2 * f + 1)
                act.wait_ge(gated, NF * n + f + START)
                nc.scalar.activation(th[:, 0:w], FB[2 * (f % 2)][:, 0:w], ACT.Tanh, scale=0.5 / X_SCALE
                                     ).then_inc(tanhed, 1)

            def hidden_hi(n, f):
                tiles = FG[f]
                act.wait_ge(gated, NF * n + f + 1 + START)
                nc.scalar.mul(hh[:, tiles[0]:tiles[-1] + 1, :].rearrange("p k t -> p (k t)"),
                              hid[:, 0:len(tiles) * P], 2.0 ** -6).then_inc(hid_hi, 1)

            def take_qk(n, c):
                act.wait_ge(qkt, 5 * n + c + 1)
                src = TR[c % 2][:, :]
                if c == 0:
                    nc.scalar.copy(kT[:, :, :].rearrange("p h t -> p (h t)"), src).then_inc(qkt_out, 1)
                else:
                    nc.scalar.copy(qT[:, c - 1, :].rearrange("p (b g t) -> p g b t", g=G, b=BT),
                                   src.rearrange("p (g b t) -> p g b t", g=G, b=BT)).then_inc(qkt_out, 1)

            take_x(0)

            def body(n, attn, ffn):
                last = isinstance(n, int) and n + 1 >= NTT
                if attn:
                    for c in range(KV):
                        square(n, c)
                if ffn:
                    act.wait_ge(xt2, n)
                    nc.scalar.copy(x2h[:, :], TR[1][:, :]).then_inc(x2_hi, 1)
                if attn:
                    square(n, KV)
                    act.wait_ge(proj, NPROJ * (n + 1))
                    nc.scalar.mul(v[:, :], PROJ[1][:, :], V_SHIFT).then_inc(v_out, 1)
                for f in range(NF):
                    for m in range(2):
                        if ffn and m == 0:
                            tanh(n - 1, f)
                        if attn:
                            for c in TRANSPOSE_AT.get((f, m), []):
                                take_qk(n, c)
                        if ffn and m == 1:
                            hidden_hi(n - 1, f)
                if attn:
                    act.wait_ge(sub, n + 1)
                    nc.scalar.activation(pr[:, :, :], sd[:, :, :], ACT.Exp).then_inc(exped, 1)
                    if not last:
                        take_x(n + 1)
                    for h in range(KV):
                        act.wait_ge(pv, KV * n + h + 1)
                        nc.scalar.copy(ch[:, G * h:G * h + G, :].rearrange("p g (b t) -> p b g t", b=BT),
                                       PV_BANK[h][:, :].rearrange("p (b g t) -> p b g t", g=G, b=BT)).then_inc(c_hi, 1)

            over_tiles(act, body)

        @block.vector
        def _(dve):
            for start in (o_out, gated, out_done):
                dve.sem_inc(start, START)
            nc.vector.memset(minus_half[:, :], -0.5).then_inc(const_set, 1)

            def ln_stats(n, m, src, var_done, self_sem):
                nc.vector.bn_stats(stats[:, m, :], src).then_inc(self_sem, 1)
                dve.wait_ge(self_sem, 3 * n + 1)
                dve.sem_inc(self_sem, 1)
                nc.vector.bn_aggr(mv[:, m, :], stats[:, m, :]).then_inc(self_sem, 1)
                dve.wait_ge(self_sem, 3 * n + 3)
                nc.vector.tensor_scalar(var[:, m, :], mv[:, m, 1:2], LN_EPS, X_SCALE ** -2, ALU.add, ALU.mult
                                        ).then_inc(var_done, 1)

            def ln_apply(n, m, src, dst, rstd_done, done):
                dve.wait_ge(rstd_done, n + 1)
                nc.vector.tensor_scalar(dst, src, mv[:, m, 0:1], rstd[:, m, :], ALU.subtract, ALU.mult
                                        ).then_inc(done, 1)

            def x_low(n):
                dve.wait_ge(x_hi, n + 1)
                nc.vector.tensor_tensor(xl[:, :], TR[0][:, :], xh[:, :], ALU.subtract).then_inc(x_lo, 1)

            def rotate(n, c):
                dve.wait_ge(squared, 5 * n + c + 1)
                if not (isinstance(n, int) and 5 * n + c < 2):
                    dve.wait_ge(added, 5 * n + c - 1)
                w = 2 if c == 0 else 0
                y = PROJ[c % 2][:, :].rearrange("p (h d) -> p h d", d=HD)
                a = ra[c % 2][:, :].rearrange("p (h d) -> p h d", d=HD)
                b = rb[c % 2][:, :].rearrange("p (h d) -> p h d", d=HD)
                half = HD // 2
                nc.vector.tensor_tensor(a, y, bcast(tables[:, w, :], [P, G, HD], 1), ALU.mult).then_inc(roped_a, 1)
                nc.vector.tensor_tensor(b[:, :, 0:half], y[:, :, half:HD],
                                        bcast(tables[:, w + 1, 0:half], [P, G, half], 1), ALU.mult
                                        ).then_inc(roped_a, 1)
                nc.vector.tensor_tensor(b[:, :, half:HD], y[:, :, 0:half],
                                        bcast(tables[:, w + 1, half:HD], [P, G, half], 1), ALU.mult
                                        ).then_inc(roped_b, 1)
                nc.vector.tensor_reduce(ss[:, G * c:G * c + G], sq[c % 2][:, :].rearrange("p (h d) -> p h d", d=HD),
                                        AX.X, ALU.add).then_inc(ssum, 1)
                dve.wait_ge(ssum, 5 * n + c + 1)
                of = slice(G * c, G * c + G)
                if c == 0:
                    nc.vector.tensor_scalar(ms[:, of], ss[:, of], 1.0 / HD, W.eps_k[:, :], ALU.mult, ALU.add
                                            ).then_inc(mean_sq, 1)
                else:
                    nc.vector.tensor_scalar(ms[:, of], ss[:, of], W.eps_q[:, :], None, ALU.add).then_inc(mean_sq, 1)

            def gate(n, f):
                w = len(FG[f]) * P
                dve.wait_ge(tanhed, NF * n + f + 1)
                dve.wait_ge(f1, 2 * NF * n + 2 * f + 2)
                nc.vector.scalar_tensor_tensor(hid[:, 0:w], th[:, 0:w], 1.0, FB[2 * (f % 2) + 1][:, 0:w],
                                               ALU.add, ALU.mult).then_inc(gated, 1)

            def hidden_lo(n, f):
                tiles = FG[f]
                dve.wait_ge(hid_hi, NF * n + f + 1)
                nc.vector.scalar_tensor_tensor(
                    hl[:, tiles[0]:tiles[-1] + 1, :].rearrange("p k t -> p (k t)"), hid[:, 0:len(tiles) * P], 2.0 ** -6,
                    hh[:, tiles[0]:tiles[-1] + 1, :].rearrange("p k t -> p (k t)"), ALU.mult, ALU.subtract
                ).then_inc(hid_lo, 1)
                dve.wait_ge(hid_lo, NF * n + f + 1)

            dve.wait_ge(ln_in, DMA)
            ln_stats(0, 0, h_ln[:, :], ln1_var, ln1_self)
            dve.wait_ge(const_in, 5 * DMA)
            nc.vector.scalar_tensor_tensor(tables[:, :, :], norm_w[:, :, :], 1.0, tables[:, :, :], ALU.add, ALU.mult
                                           ).then_inc(const_set, 1)
            ln_apply(0, 0, h_ln[:, :], xn[:, :], ln1_rstd, ln1)
            dve.wait_ge(const_set, 2)
            x_low(0)

            def body(n, attn, ffn):
                last = isinstance(n, int) and n + 1 >= NTT
                if attn:
                    rotate(n, 0)
                if ffn:
                    ln_apply(n - 1, 1, h2[:, :], x2n[:, :], ln2_rstd, ln2)
                if attn:
                    for c in range(1, KV):
                        rotate(n, c)
                if ffn:
                    dve.wait_ge(x2_hi, n)
                    nc.vector.tensor_tensor(x2l[:, :], TR[1][:, :], x2h[:, :], ALU.subtract).then_inc(x2_lo, 1)
                if attn:
                    rotate(n, KV)
                    if not last:
                        dve.wait_ge(ln_in, DMA * (n + 2))
                        ln_stats(n + 1, 0, h_ln[:, :], ln1_var, ln1_self)
                if ffn:
                    for f in range(2):
                        gate(n - 1, f)
                        hidden_lo(n - 1, f)
                if attn:
                    if not last:
                        ln_apply(n + 1, 0, h_ln[:, :], xn[:, :], ln1_rstd, ln1)
                    step = [0]

                    def link(ins):
                        step[0] += 1
                        ins.then_inc(soft, 1)
                        dve.wait_ge(soft, 4 * n + step[0])

                    dve.wait_ge(scored, n + 1)
                    nc.vector.tensor_tensor(sm[:, :, :], SCORES[:, :].rearrange("p (u k) -> p u k", k=SEQ),
                                            bcast(mask[:, :], [P, HEADS, SEQ], 1), ALU.add).then_inc(masked, 1)
                    dve.wait_ge(masked, n + 1)
                    link(nc.vector.tensor_reduce(mx[:, :], sm[:, :, :], AX.X, ALU.max))
                    nc.vector.tensor_tensor(sd[:, :, :], sm[:, :, :], bcast(mx[:, :], [P, HEADS, SEQ], 2),
                                            ALU.subtract).then_inc(sub, 1)
                if ffn:
                    gate(n - 1, 2)
                if attn:
                    dve.wait_ge(exped, n + 1)
                    link(nc.vector.tensor_reduce(den[:, :], pr[:, :, :], AX.X, ALU.add))
                    link(nc.vector.reciprocal(rden[:, :], den[:, :]))
                    link(nc.vector.tensor_tensor(pr[:, :, :], pr[:, :, :], bcast(rden[:, :], [P, HEADS, SEQ], 2),
                                                 ALU.mult))
                if ffn:
                    hidden_lo(n - 1, 2)
                if attn:
                    dve.wait_ge(pt, n + 1)
                    for h in range(KV):
                        nc.vector.tensor_tensor(pbd[:, h, :, :],
                                                bcast(TR[1][:, h * P:(h + 1) * P], [P, BT, G * SEQ], 1),
                                                bcast(own[:, :], [P, BT, G * SEQ], 2), ALU.mult).then_inc(pbd_out, 1)
                        if h == 1 and not last:
                            x_low(n + 1)
                if attn:
                    for h in range(KV):
                        dve.wait_ge(c_hi, KV * n + h + 1)
                        nc.vector.tensor_tensor(cl[:, G * h:G * h + G, :].rearrange("p g (b t) -> p b g t", b=BT),
                                                PV_BANK[h][:, :].rearrange("p (b g t) -> p b g t", g=G, b=BT),
                                                ch[:, G * h:G * h + G, :].rearrange("p g (b t) -> p b g t", b=BT),
                                                ALU.subtract).then_inc(c_lo, 1)
                if ffn:
                    dve.wait_ge(w3, n)
                    dve.wait_ge(out_done, DMA * (n - 1) + START)
                    nc.vector.scalar_tensor_tensor(o_tile[:, :], PROJ[0][:, :], 2.0 ** -6, h2[:, :], ALU.mult, ALU.add
                                                   ).then_inc(o_out, 1)
                if attn:
                    dve.wait_ge(o_sum, n + 1)
                    if ffn:
                        dve.wait_ge(o_out, n + START)
                    dve.wait_ge(res_in, DMA * (n + 1))
                    nc.vector.scalar_tensor_tensor(h2[:, :], PROJ[1][:, :], W.o_unscale[:, :], h_res[:, :], ALU.mult,
                                                   ALU.add).then_inc(h2_done, 1)
                    dve.wait_ge(h2_done, n + 1)
                    ln_stats(n, 1, h2[:, :], ln2_var, ln2_self)

            over_tiles(dve, body)

        @block.tensor
        def _(pe):
            pe.wait_ge(const_in, 5 * DMA)

            def transpose(dst, src, last_sem):
                for k in range(KD):
                    t = nc.tensor.transpose(dst[:, k * P:(k + 1) * P], src[:, k * P:(k + 1) * P], ident[:, :])
                t.then_inc(last_sem, 1)

            def split_products(dst, pairs, done):
                for i, (ah, al, bh, bl) in enumerate(pairs):
                    nc.tensor.matmul(dst, ah, bh, start=(i == 0), stop=False)
                    nc.tensor.matmul(dst, ah, bl, start=False, stop=False)
                    t = nc.tensor.matmul(dst, al, bh, start=False, stop=(i == len(pairs) - 1))
                t.then_inc(done, 1)

            def project(n, c, first):
                if c == 0 and not first:
                    pe.wait_ge(o_out, n - 1 + START)
                if c == 1:
                    pe.wait_ge(h2_done, n)
                if c >= 2:
                    pe.wait_ge(squared, 5 * n + c - 1)
                    pe.wait_ge(roped_b, 5 * n + c - 1)
                pairs = []
                for k in range(KD):
                    at = (K_AT + k * KV * HD if c == 0 else V_AT + k * KV * HD if c == NPROJ - 1
                          else Q_AT + k * HEADS * HD + (c - 1) * D)
                    pairs.append((xh[:, k * P:(k + 1) * P], xl[:, k * P:(k + 1) * P],
                                  W.a_hi[:, at:at + D], W.a_lo[:, at:at + D]))
                split_products(PROJ[c % 2][:, :], pairs, proj)

            def transpose_x(n):
                pe.wait_ge(ln1, n + 1)
                pe.wait_ge(qkt_out, 5 * n)
                transpose(TR[0], xn, xt)

            def transpose_x2(n):
                pe.wait_ge(ln2, n + 1)
                pe.wait_ge(pbd_out, KV * (n + 1))
                transpose(TR[1], x2n, xt2)

            def gate_products(n, f, m):
                if f == 0 and m == 0:
                    pe.wait_ge(ffn_in, 3 * DMA)
                    pe.wait_ge(x2_hi, n + 1)
                    pe.wait_ge(x2_lo, n + 1)
                    pe.wait_ge(c_hi, KV * (n + 1))
                    pe.wait_ge(c_lo, KV * (n + 1))
                    pe.wait_ge(masked, n + 1)
                if f == 2:
                    pe.wait_ge(gated, NF * n + 1 + START)
                for j, t in enumerate(FG[f]):
                    for k in range(KD):
                        at = (m * KD + k) * FF + t * P
                        w = ffn_w[:, at:at + P]
                        dst = FB[2 * (f % 2) + m][:, j * P:(j + 1) * P]
                        nc.tensor.matmul(dst, w, x2h[:, k * P:(k + 1) * P], start=(k == 0), stop=False)
                        ins = nc.tensor.matmul(dst, w, x2l[:, k * P:(k + 1) * P], start=False, stop=(k == KD - 1))
                ins.then_inc(f1, 1)

            def transpose_qk(n, c, ffn):
                pe.wait_ge(q_ready, 5 * n + c + 1)
                if c == 1 and ffn:
                    pe.wait_ge(x2_lo, n)
                if c >= 2:
                    pe.wait_ge(qkt_out, 5 * n + c - 1)
                transpose(TR[c % 2], rope[:, c, :], qkt)

            def scores(n, ffn):
                pe.wait_ge(qkt_out, 5 * n + 5)
                if ffn:
                    pe.wait_ge(gated, NF * (n - 1) + 2 + START)
                for h in range(KV):
                    for b in range(BT):
                        at = h * P + b * SEQ
                        ins = nc.tensor.matmul(SCORES[:, at:at + SEQ], qT[:, h, b * P:(b + 1) * P],
                                               kT[:, h, b * SEQ:(b + 1) * SEQ], start=True, stop=True)
                ins.then_inc(scored, 1)

            def down_products(n, tiles):
                if tiles[0] == 0:
                    if isinstance(n, int) and n + 1 >= NTT:
                        pe.wait_ge(o_out, n + START)
                    else:
                        pe.wait_ge(squared, 5 * (n + 1) + 5)
                        pe.wait_ge(roped_b, 5 * (n + 1) + 5)
                for k in tiles:
                    if k == 0 or k in (FG[1][0], FG[2][0]):
                        f = [g[0] for g in FG].index(k)
                        pe.wait_ge(hid_hi, NF * n + f + 1)
                        pe.wait_ge(hid_lo, NF * n + f + 1)
                    at = 2 * KD * FF + k * D
                    nc.tensor.matmul(PROJ[0][:, :], hh[:, k, :], ffn_w[:, at:at + D], start=(k == 0), stop=False)
                    ins = nc.tensor.matmul(PROJ[0][:, :], hl[:, k, :], ffn_w[:, at:at + D], start=False,
                                           stop=(k == KF - 1))
                if tiles[-1] == KF - 1:
                    ins.then_inc(w3, 1)

            def weigh_values(n, ffn):
                pe.wait_ge(v_out, n + 1)
                for h in range(KV):
                    pe.wait_ge(pbd_out, KV * n + h + 1)
                    if h == 0 and ffn:
                        pe.wait_ge(gated, NF * n + START)
                    if h == KV - 1:
                        pe.wait_ge(c_lo, KV * n + 1)
                    nc.tensor.matmul(PV_BANK[h][:, :], v[:, h * HD:(h + 1) * HD],
                                     pbd[:, h, :, :].rearrange("p b q -> p (b q)"), start=True, stop=True
                                     ).then_inc(pv, 1)

            def output_products(n):
                for k in range(HEADS):
                    if k % G == 0:
                        pe.wait_ge(c_hi, KV * n + k // G + 1)
                        pe.wait_ge(c_lo, KV * n + k // G + 1)
                    at = O_AT + k * D
                    ah, al = ch[:, k, :], cl[:, k, :]
                    bh, bl = W.a_hi[:, at:at + D], W.a_lo[:, at:at + D]
                    nc.tensor.matmul(PROJ[1][:, :], ah, bh, start=(k == 0), stop=False)
                    nc.tensor.matmul(PROJ[1][:, :], ah, bl, start=False, stop=False)
                    ins = nc.tensor.matmul(PROJ[1][:, :], al, bh, start=False, stop=(k == HEADS - 1))
                ins.then_inc(o_sum, 1)

            transpose_x(0)

            def body(n, attn, ffn):
                last = isinstance(n, int) and n + 1 >= NTT
                if attn:
                    pe.wait_ge(x_hi, n + 1)
                    pe.wait_ge(x_lo, n + 1)
                    for c in range(NPROJ - 2):
                        project(n, c, isinstance(n, int) and n == 0)
                if ffn:
                    transpose_x2(n - 1)
                if attn:
                    for c in range(NPROJ - 2, NPROJ):
                        project(n, c, False)
                for f in range(NF):
                    for m in range(2):
                        if ffn:
                            gate_products(n - 1, f, m)
                        if attn:
                            for c in TRANSPOSE_AT.get((f, m), []):
                                transpose_qk(n, c, ffn)
                            if (f, m) == SCORES_AT:
                                scores(n, ffn)
                if ffn:
                    down_products(n - 1, range(0, DOWN_FIRST))
                if attn and not last:
                    transpose_x(n + 1)
                if attn:
                    pe.wait_ge(soft, 4 * n + 4)
                    transpose(TR[1], pr[:, :, :].rearrange("p u k -> p (u k)"), pt)
                if ffn:
                    down_products(n - 1, range(DOWN_FIRST, KF))
                if attn:
                    weigh_values(n, ffn)
                    output_products(n)

            over_tiles(pe, body)


def program(nc, x, vt, w_attn, w_ffn, tables, norm_w, mask, own, ident, out):
    h1 = nc.dram_tensor("h1_rows", (TOK, D), FP32, kind="Internal").ap()
    ffn_store = nc.dram_tensor("ffn_ternary", (P, FFN_W), F16, kind="Internal").ap()
    with ExitStack() as ctx:
        W = Weights(lambda name, shape, dt=FP32: ctx.enter_context(nc.sbuf_tensor(name, shape, dt)))
        token_attention(nc, x, vt, h1, ident, W, w_attn, w_ffn, ffn_store)
        blocks(nc, W, ffn_store, h1, tables, norm_w, mask, own, ident, out)


_OUTS = [((B, CH, T), "float32")]


def _constants():
    inv_freq = (1.0 / np.float32(10000.0) ** (np.arange(0, HD, 2, dtype=np.float32) / HD)).astype(np.float32)
    freqs = np.arange(SEQ, dtype=np.float32)[:, None] * inv_freq[None, :]
    emb = np.concatenate([freqs, freqs], axis=-1)
    cos, sin = np.cos(emb).astype(np.float32), np.sin(emb).astype(np.float32)
    sin[:, :HD // 2] *= -1.0
    rotary = np.tile(np.stack([cos, sin, cos, sin], axis=1), (BT, 1, 1))
    t = np.arange(P)[:, None] % SEQ
    mask = np.where(np.arange(SEQ)[None, :] <= t, 0.0, -1e30).astype(np.float32)
    own = (np.arange(P)[:, None] // SEQ == np.arange(BT)[None, :]).astype(np.float32)
    return rotary.astype(np.float32), mask, own, np.eye(P, dtype=np.float32)


def _tiled(w):
    return w.reshape(-1, P, w.shape[1]).transpose(1, 0, 2).reshape(P, -1)


def kernel(**inputs):
    import concourse.bacc as _bacc
    from concourse.bass_utils import run_bass_kernel_spmd as _run

    a = {k: np.asarray(v) for k, v in inputs.items()}
    rotary, mask, own, ident = _constants()
    v = a["x"][:, 2 * CH:].reshape(NG, GB, CH, NT, P)
    qn, kn = a["L0_attn_qn_w"], a["L0_attn_kn_w"]
    halves = [np.concatenate([w[HD // 2:], w[:HD // 2]]) for w in (qn, kn)]
    arrays = {
        "x": a["x"],
        "v_t": v.transpose(0, 4, 3, 1, 2).reshape(NG, P, T),
        "w_attn": np.concatenate([_tiled(a[f"L0_attn_{n}"].T) for n in ("Wq", "Wk", "Wv", "Wo")], axis=1),
        "w_ffn": np.concatenate([_tiled(a[f"L0_ffn_{n}"].T) for n in ("w1", "w2", "w3")], axis=1),
        "rotary": rotary,
        "norm_weights": np.broadcast_to(np.stack([qn, halves[0], kn, halves[1]]), (P, 4, HD)),
        "causal": mask,
        "own": own,
        "identity": ident,
    }
    arrays = {k: np.ascontiguousarray(v) for k, v in arrays.items()}
    nc = _bacc.Bacc("TRN2", target_bir_lowering=False, num_devices=1)
    args = [nc.dram_tensor(f"in_{k}", v.shape, mybir.dt.from_np(v.dtype), kind="ExternalInput").ap()
            for k, v in arrays.items()]
    out = nc.dram_tensor("out", _OUTS[0][0], FP32, kind="ExternalOutput").ap()
    program(nc, *args, out.rearrange("b c t -> (b c) t"))
    r = _run(nc, [{f"in_{k}": v for k, v in arrays.items()}], core_ids=[0])
    return r.results[0]["out"]
```
